# Optimizing a Trainium2 kernel written in Bass

```python
import numpy as np
import jax
import jax.numpy as jnp

def _softmax(x, axis=-1):
    return jax.nn.softmax(x, axis=axis)

def _gelu(x):
    return jax.nn.gelu(x, approximate=True)

def _silu(x):
    return jax.nn.silu(x)

def _sigmoid(x):
    return jax.nn.sigmoid(x)

def _layernorm(x, axis=-1, eps=1e-05):
    m = jnp.mean(x, axis=axis, keepdims=True)
    v = jnp.var(x, axis=axis, keepdims=True)
    return (x - m) / jnp.sqrt(v + eps)

def _scatter_add(tgt, idx, src, axis=0):
    return tgt.at[idx].add(src)

def _segment_sum(src, seg, n):
    return jax.ops.segment_sum(src, seg, n)
kernel_name = 'mk_gnn_preln_d2_gnn_r8_ffd22e'

def setup_inputs(seed: int=0):
    np.random.seed(seed)
    _w = jnp.asarray

    def _rec_inputs():
        import jax
        import jax.numpy as jnp
        _gk = jax.random.key(seed)
        x = -0.000202 + 1 * jax.random.normal(jax.random.fold_in(_gk, 1), (6250, 128), jnp.float32)
        src = jax.random.randint(jax.random.fold_in(_gk, 2), (200000,), 0, 6250, jnp.int32)
        dst = jax.random.randint(jax.random.fold_in(_gk, 3), (200000,), 0, 6250, jnp.int32)
        _o = jnp.argsort(dst, stable=True)
        src = src[_o]
        dst = dst[_o]
        edge_attr_4 = -0.000107899 + 1.00008 * jax.random.normal(jax.random.fold_in(_gk, 12), (200000, 4), jnp.float32)
        edge_attr_8 = jax.random.uniform(jax.random.fold_in(_gk, 13), (200000, 8), jnp.float32, 0.0, 1)
        return (x, src, dst, edge_attr_4, edge_attr_8)
    x, src, dst, edge_attr_4, edge_attr_8 = _rec_inputs()

    def _L0_gnn_setup():
        import jax, jax.numpy as jnp
        import numpy as np
        N_NODES = 6250
        N_EDGES = 200000
        HIDDEN = 128
        HEADS = 8
        PER_HEAD = HIDDEN // HEADS
        NEG_SLOPE = 0.2
        key = jax.random.key(seed)
        ks = jax.random.split(key, 7)
        feat = jax.random.normal(ks[0], (N_NODES, HIDDEN), dtype=jnp.float32)
        src = jax.random.randint(ks[1], (N_EDGES,), 0, N_NODES, dtype=jnp.int32)
        dst = jax.random.randint(ks[2], (N_EDGES,), 0, N_NODES, dtype=jnp.int32)
        W = jax.random.normal(ks[3], (HIDDEN, HEADS * PER_HEAD), dtype=jnp.float32) / np.sqrt(HIDDEN)
        attn_l = jax.random.normal(ks[4], (HEADS, PER_HEAD), dtype=jnp.float32) / np.sqrt(PER_HEAD)
        attn_r = jax.random.normal(ks[5], (HEADS, PER_HEAD), dtype=jnp.float32) / np.sqrt(PER_HEAD)
        bias = jnp.zeros((HEADS * PER_HEAD,), dtype=jnp.float32)
        return {'feat': feat, 'src': src, 'dst': dst, 'W': W, 'attn_l': attn_l, 'attn_r': attn_r, 'bias': bias}
    _L0_gnn_all = _L0_gnn_setup()
    _L0_gnn_in = {k: v for k, v in _L0_gnn_all.items() if k in ('W', 'attn_l', 'attn_r', 'bias')}
    del _L0_gnn_all

    def _L1_gnn_setup():
        import jax, jax.numpy as jnp
        import numpy as np
        MUL = 32
        N_NODES = 6250
        N_EDGES = 100000
        R3 = np.sqrt(3.0).astype(np.float32)
        key = jax.random.key(seed)
        ks = jax.random.split(key, 12)
        inp = {}
        inp['node_feats'] = jax.random.normal(ks[0], (N_NODES, 4 * MUL), dtype=jnp.float32)
        inp['edge_attrs'] = jax.random.normal(ks[1], (N_EDGES, 4), dtype=jnp.float32)
        inp['edge_feats'] = jax.random.uniform(ks[2], (N_EDGES, 8), dtype=jnp.float32)
        inp['edge_index'] = jax.random.randint(ks[3], (2, N_EDGES), 0, N_NODES)
        inp['W_up_s'] = jax.random.normal(ks[4], (MUL, MUL), dtype=jnp.float32)
        inp['W_up_v'] = jax.random.normal(ks[5], (MUL, MUL), dtype=jnp.float32)
        inp['A1'] = jax.random.normal(ks[6], (8, 64), dtype=jnp.float32) / np.sqrt(8.0)
        inp['b1'] = jnp.zeros((64,), dtype=jnp.float32)
        inp['A2'] = jax.random.normal(ks[7], (64, 64), dtype=jnp.float32) / np.sqrt(64.0)
        inp['b2'] = jnp.zeros((64,), dtype=jnp.float32)
        inp['A3'] = jax.random.normal(ks[8], (64, 4 * MUL), dtype=jnp.float32) * (10.0 * np.sqrt(6.0 / (64 + 4 * MUL)))
        inp['W_out_s'] = jax.random.normal(ks[9], (2 * MUL, MUL), dtype=jnp.float32)
        inp['W_out_v'] = jax.random.normal(ks[10], (2 * MUL, MUL), dtype=jnp.float32)
        return inp
    _L1_gnn_all = _L1_gnn_setup()
    _L1_gnn_in = {k: v for k, v in _L1_gnn_all.items() if k in ('W_up_s', 'W_up_v', 'A1', 'b1', 'A2', 'b2', 'A3', 'W_out_s', 'W_out_v')}
    del _L1_gnn_all
    return {'x': x, 'src': src, 'dst': dst, 'edge_attr_4': edge_attr_4, 'edge_attr_8': edge_attr_8, 'L0_gnn_W': _L0_gnn_in['W'], 'L0_gnn_attn_l': _L0_gnn_in['attn_l'], 'L0_gnn_attn_r': _L0_gnn_in['attn_r'], 'L0_gnn_bias': _L0_gnn_in['bias'], 'L1_gnn_W_up_s': _L1_gnn_in['W_up_s'], 'L1_gnn_W_up_v': _L1_gnn_in['W_up_v'], 'L1_gnn_A1': _L1_gnn_in['A1'], 'L1_gnn_b1': _L1_gnn_in['b1'], 'L1_gnn_A2': _L1_gnn_in['A2'], 'L1_gnn_b2': _L1_gnn_in['b2'], 'L1_gnn_A3': _L1_gnn_in['A3'], 'L1_gnn_W_out_s': _L1_gnn_in['W_out_s'], 'L1_gnn_W_out_v': _L1_gnn_in['W_out_v']}

def reference(x, src, dst, edge_attr_4, edge_attr_8, L0_gnn_W, L0_gnn_attn_l, L0_gnn_attn_r, L0_gnn_bias, L1_gnn_W_up_s, L1_gnn_W_up_v, L1_gnn_A1, L1_gnn_b1, L1_gnn_A2, L1_gnn_b2, L1_gnn_A3, L1_gnn_W_out_s, L1_gnn_W_out_v):
    import jax
    import jax.numpy as jnp

    def _L0_gnn_ref(feat, src, dst, W, attn_l, attn_r, bias):
        import jax, jax.numpy as jnp
        import numpy as np
        N_NODES = 6250
        N_EDGES = 200000
        HIDDEN = 128
        HEADS = 8
        PER_HEAD = HIDDEN // HEADS
        NEG_SLOPE = 0.2
        N = feat.shape[0]
        z = (feat @ W).reshape(N, HEADS, PER_HEAD)
        el = jnp.einsum('nhp,hp->nh', z, attn_l)
        er = jnp.einsum('nhp,hp->nh', z, attn_r)
        e = jax.nn.leaky_relu(el[src] + er[dst], negative_slope=NEG_SLOPE)
        emax = jax.ops.segment_max(e, dst, num_segments=N)
        emax = jnp.where(jnp.isfinite(emax), emax, 0.0)
        a = jnp.exp(e - emax[dst])
        denom = jax.ops.segment_sum(a, dst, num_segments=N)
        msg = z[src] * a[:, :, None]
        agg = jax.ops.segment_sum(msg, dst, num_segments=N)
        out = agg / jnp.maximum(denom, 1e-09)[:, :, None]
        out = out + bias.reshape(1, HEADS, PER_HEAD)
        return out.reshape(N, HEADS * PER_HEAD)

    def _L1_gnn_ref(node_feats, edge_attrs, edge_feats, W_up_s, W_up_v, A1, b1, A2, b2, A3, W_out_s, W_out_v, edge_index):
        import jax, jax.numpy as jnp
        import numpy as np
        MUL = 32
        N_NODES = 6250
        N_EDGES = 100000
        R3 = np.sqrt(3.0).astype(np.float32)
        num_nodes = node_feats.shape[0]
        sender, receiver = (edge_index[0], edge_index[1])
        s = node_feats[:, :MUL]
        v = node_feats[:, MUL:].reshape(num_nodes, MUL, 3)
        inv = 1.0 / np.sqrt(MUL).astype(np.float32)
        s = s @ W_up_s * inv
        v = jnp.einsum('nui,uw->nwi', v, W_up_v) * inv
        h = jax.nn.silu(edge_feats @ A1 + b1)
        h = jax.nn.silu(h @ A2 + b2)
        tpw = h @ A3
        w0, w1, w2, w3 = jnp.split(tpw, 4, axis=1)
        ss = s[sender]
        vs = v[sender]
        y_s = edge_attrs[:, :1]
        y_v = edge_attrs[:, 1:4]
        out_s0 = ss * y_s * w0
        out_s3 = jnp.einsum('eui,ei->eu', vs, y_v) / R3 * w3
        out_v1 = ss[:, :, None] * y_v[:, None, :] * w1[:, :, None]
        out_v2 = vs * y_s[:, :, None] * w2[:, :, None]
        E = ss.shape[0]
        mji = jnp.concatenate([out_s0, out_s3, out_v1.reshape(E, 3 * MUL), out_v2.reshape(E, 3 * MUL)], axis=1)
        message = jax.ops.segment_sum(mji, receiver, num_segments=num_nodes) / 10.0
        ms = message[:, :2 * MUL]
        mv = message[:, 2 * MUL:].reshape(num_nodes, 2 * MUL, 3)
        inv2 = 1.0 / np.sqrt(2 * MUL).astype(np.float32)
        out_s = ms @ W_out_s * inv2
        out_v = jnp.einsum('nui,uw->nwi', mv, W_out_v) * inv2
        return jnp.concatenate([out_s, out_v.reshape(num_nodes, 3 * MUL)], axis=1)
    edge_index = jnp.stack([src, dst])
    h = jnp.maximum(_layernorm(x, axis=-1), 0.0)
    x = x + _L0_gnn_ref(h, src, dst, L0_gnn_W, L0_gnn_attn_l, L0_gnn_attn_r, L0_gnn_bias)
    h = jnp.maximum(_layernorm(x, axis=-1), 0.0)
    x = x + _L1_gnn_ref(h, edge_attr_4, edge_attr_8, L1_gnn_W_up_s, L1_gnn_W_up_v, L1_gnn_A1, L1_gnn_b1, L1_gnn_A2, L1_gnn_b2, L1_gnn_A3, L1_gnn_W_out_s, L1_gnn_W_out_v, edge_index)
    return x

_drawn_inputs = setup_inputs


def setup_inputs(seed=0):
    import zlib

    import numpy as np

    out = dict(_drawn_inputs(seed))
    spreads = {'L0_gnn_bias': (0.0, 0.1), 'L1_gnn_b1': (0.0, 0.1), 'L1_gnn_b2': (0.0, 0.1)}
    factors = {}
    for name, (base, spread) in spreads.items():
        noise = np.random.default_rng([zlib.crc32(name.encode()), seed]).standard_normal(out[name].shape)
        drawn = base * np.exp(spread * noise) if base else spread * noise
        out[name] = jnp.asarray(drawn.astype(out[name].dtype))
    for name, factor in factors.items():
        out[name] = (out[name] * factor).astype(out[name].dtype)
    return out
```

```python
from contextlib import ExitStack

import concourse.bass as bass
from concourse import mybir

F32 = mybir.dt.float32
I32 = mybir.dt.int32
ALU = mybir.AluOpType
ACT = mybir.ActivationFunctionType
AX = mybir.AxisListType

P = 128
NODES, EDGES, HIDDEN, HEADS, MUL = 6250, 200000, 128, 8, 32
PER_HEAD = HIDDEN // HEADS
NEG_SLOPE = 0.2
EPS = 1e-5

NB = -(-NODES // P)
BU = 7
BI = NB // BU
TAIL = NODES - (NB - 1) * P
COLS = (NB + 1) * P
PAD_DST = COLS - 1

T = 8
HT = T // 2
GE = T * P
NG = EDGES // GE + 1
U = 4
GI = NG // U
WIN = 64
PASSES = -(-NODES // WIN)
SPREAD = 80.0
TINY = 1e-36
ZW = HIDDEN + HEADS

assert NB == BU * BI and NG == U * GI and NG * GE >= EDGES and PAD_DST >= NODES + WIN


def bc(ap, axis, n):
    wide = ap.unsqueeze(axis)
    shape = list(wide.shape)
    shape[axis] = n
    return wide.broadcast_to(shape)


def gnn_kernel(nc, x, src, dst, edge_y, edge_f, W, attn_l, attn_r, bias, W_up_s, W_up_v, A1, b1, A2, b2, A3,
               W_out_s, W_out_v, identity, out):
    with ExitStack() as ctx:
        def sb(name, shape, dt=F32):
            return ctx.enter_context(nc.sbuf_tensor(name, shape, dt))

        def sem(name):
            return ctx.enter_context(nc.semaphore(name))

        def sems(name, n):
            return [sem(f"{name}{i}") for i in range(n)]

        def dram(name, shape, dt=F32):
            return nc.dram_tensor(name, shape, dt, kind="Internal").ap()

        z_tab = dram("z_tab", (NB * P, ZW))
        er_tab = dram("er_tab", (COLS, 2 * HEADS))
        up_tab = dram("up_tab", (NB * P, HIDDEN))
        win_dram = dram("win_dram", (2 * NG,))
        top_dram = dram("top_dram", (2 * HEADS,))

        bank = [ctx.enter_context(nc.psum_tensor(f"bank{i}", [P, 512], F32)) for i in range(8)]

        x_sb = sb("x_sb", [P, NB, HIDDEN])
        acc_a = sb("acc_a", [P, COLS])
        acc_b = sb("acc_b", [P, 3, COLS])
        den_acc = acc_b[0:HEADS, 0, :]
        max_acc = acc_b[0:HEADS, 1, :]
        dst_rel = sb("dst_rel", [P, NG, T])
        win_f = sb("win_f", [P, NG])
        win_i = sb("win_i", [1, NG], I32)
        ident = sb("ident", [P, P])
        iota = sb("iota", [P, WIN])
        flags = sb("flags", [P, 8])
        flags_i = sb("flags_i", [1, 2], I32)
        vec = sb("vec", [P, 8])
        bias_bc = sb("bias_bc", [P, HIDDEN])
        w_aug = sb("w_aug", [P, 144])
        w_up = sb("w_up", [P, HIDDEN])
        a1_bd = sb("a1_bd", [16, P])
        a2_bd = sb("a2_bd", [P, P])
        a3_bd = sb("a3_bd", [P, 2 * P])
        wo_a = sb("wo_a", [P, HIDDEN])
        wo_b = sb("wo_b", [P, 3, HIDDEN])
        rows = sb("rows", [P, U, T, ZW])
        idx = sb("idx", [P, U, T], I32)
        er_win = sb("er_win", [P, U, 4 * HEADS])
        y_sb = sb("y_sb", [P, U, T, 4])
        ef_sb = sb("ef_sb", [16, U, HT * P])

        share = sb("share", [P, 7168])

        def part(at, *shape, parts=P):
            n = 1
            for s in shape:
                n *= s
            flat = share[0:parts, at:at + n]
            names = "abcd"[:len(shape)]
            if len(shape) == 1:
                return flat
            return flat.rearrange(f"p ({' '.join(names)}) -> p {' '.join(names)}",
                                  **{c: s for c, s in zip(names[1:], shape[1:])})

        h_sb = part(0, BU, P)
        hT_sb = part(896, BU, P)
        row_sb = part(1792, BU, 144)
        stats = part(2800, BU, 6)
        mv = part(2842, BU, 2)
        std = part(2856, BU)
        rstd = part(2863, BU)
        nmr = part(2870, BU)
        rden = part(2877, BU * HEADS)
        elr = part(3000, NB, 2 * HEADS)
        erm = part(3784, NB, 2 * HEADS)
        top = part(4568, NB, HEADS)
        dst_i = part(4960, NG, T).bitcast(I32)
        redn = part(6528, 2, NG)
        wide = part(6528, 2 * NG)
        cols4 = part(6920, 4, parts=98)
        top16 = part(6924, 2 * HEADS)
        top_bc = part(6940, 2 * HEADS)
        wT = part(6960, P)
        attn_bd = part(7088, 2 * HEADS)
        stage_max = part(2048, P, parts=HEADS)
        elT_sb = part(0, GE, parts=HEADS)
        dst_row = part(1024, GE, parts=1).bitcast(I32)
        hot = part(0, 2, T, WIN)
        hotT = part(1024, 2, 512)
        msg = part(2048, 2, T, P)
        e_sb = part(4096, 4, T * HEADS)
        a_sb = part(4352, 2, T, HEADS)
        eq = part(0, 2, HT, WIN)
        wy = part(512, 2, HT, 4 * WIN)
        prod = part(2560, 2, HT, 2, P)
        h1_sb = part(4608, 512)
        h2_sb = part(5120, 2, 512)
        stage = part(1792, BU, 4, P)

        loads = {n: sem(f"load_{n}") for n in
                 ("x", "const", "dst", "w", "attn", "bias", "mlp", "up", "out_w", "win", "top")}
        zeroed = sem("zeroed")
        step = {e: sem(f"own_{e}") for e in ("act", "dve")}
        wait_for = {n: sem(n) for n in (
            "red_ready", "red_turned", "cols_ready", "win_stored", "wT_ready", "wT_copied", "attn_ready", "wa_ready",
            "w_ready", "top_ready", "top_turned", "top_stored", "flags_ready", "er_stored", "er_ready_tab",
            "pass_set", "out_w_ready", "up_w_ready")}

        def node_sems(tag):
            return {n: sem(f"{tag}_{n}") for n in
                    ("var", "std", "stat", "norm", "turned", "turned_sb", "lin", "lin_free", "row", "stored",
                     "agg_staged", "agg", "agg_used", "added")}

        s_in, s_mid, s_out = node_sems("in"), node_sems("mid"), node_sems("out")

        def edge_sems(tag):
            one = {n: sem(f"{tag}_{n}") for n in
                   ("rows_free", "hot", "turned", "hot_turned", "er", "score", "exp", "msg", "agg", "added",
                    "h1", "h1_act", "h2", "h2_act", "tp", "prod", "half_free")}
            one |= {n: sems(f"{tag}_{n}_slot", U) for n in ("idx", "rows", "in")}
            return one

        s_l1, s_l2 = edge_sems("l1"), edge_sems("l2")
        s_max = {n: sem(f"max_{n}") for n in ("idx", "rows", "dst", "free", "turned", "taken", "col", "staged", "blk",
                                              "top")}

        block = ctx.enter_context(nc.Block())
        G = wait_for

        passed = sem("passed")

        def plain_wait(eng, s, value):
            eng.wait_ge(s, value)

        def hold(eng, s, value):
            eng.wait_ge(s, value)
            eng.sem_inc(passed, 1)

        class Own:

            def __init__(self, eng, s):
                self.eng, self.s, self.n, self.base = eng, s, 0, None

            def after(self, ins, wait=None):
                ins.then_inc(self.s, 1)
                self.n += 1
                (wait or plain_wait)(self.eng, self.s, self.n if self.base is None else self.base + self.n)

        @block.sync
        def _(sp):
            sp.dma_start(dst_i, dst.rearrange("g p t -> p g t")).then_inc(loads["dst"], 16)
            sp.dma_start(ident[:, :], identity[:, 0:P]).then_inc(loads["const"], 16)
            sp.dma_start(iota[:, :], identity[:, P:P + WIN]).then_inc(loads["const"], 16)
            sp.dma_start(w_aug[:, 0:HIDDEN], W).then_inc(loads["w"], 16)
            for n, a in enumerate((attn_l, attn_r)):
                sp.dma_start(vec[:, n:n + 1], a.rearrange("h (p a) -> (h p) a", a=1)).then_inc(loads["attn"], 16)
            for c in range(BI):
                sp.dma_start(x_sb[:, c * BU:(c + 1) * BU, :],
                             x[c * BU * P:(c + 1) * BU * P, :].rearrange("(k p) f -> p k f", p=P))\
                  .then_inc(loads["x"], 16)
            sp.dma_start(bias_bc[:, :], bias.partition_broadcast(P)).then_inc(loads["bias"], 16)
            sp.wait_ge(zeroed, 7)
            for half in range(2):
                sp.dma_start(a1_bd[8 * half:8 * half + 8, 64 * half:64 * half + 64], A1).then_inc(loads["mlp"], 16)
                sp.dma_start(a2_bd[64 * half:64 * half + 64, 64 * half:64 * half + 64], A2).then_inc(loads["mlp"], 16)
                sp.dma_start(a3_bd[64 * half:64 * half + 64, P * half:P * half + P], A3).then_inc(loads["mlp"], 16)
                for n, b in enumerate((b1, b2)):
                    sp.dma_start(vec[64 * half:64 * half + 64, 2 + n:3 + n], b.rearrange("(n a) -> n a", a=1))\
                      .then_inc(loads["mlp"], 16)
            sp.dma_start(w_up[0:MUL, 96:128], W_up_s).then_inc(loads["up"], 16)
            sp.dma_start(wo_a[96:128, 0:MUL], W_out_s[0:MUL, :]).then_inc(loads["out_w"], 16)
            for i in range(3):
                sp.dma_start(w_up[MUL + i:P:3, MUL * i:MUL * i + MUL], W_up_v).then_inc(loads["up"], 16)
                vcols = wo_a[MUL * i:MUL * i + MUL, MUL + i:P:3]
                sp.dma_start(vcols, W_out_v[MUL:2 * MUL, :], allow_slow_non_contiguous=True).then_inc(loads["out_w"], 16)
                sp.dma_start(wo_b[MUL * i:MUL * i + MUL, i, 0:MUL], W_out_s[MUL:2 * MUL, :])\
                  .then_inc(loads["out_w"], 16)
                sp.dma_start(wo_b[96:128, i, MUL + i:P:3], W_out_v[0:MUL, :],
                             allow_slow_non_contiguous=True).then_inc(loads["out_w"], 16)

            sp.wait_ge(G["cols_ready"], 1)
            for n, c in enumerate(cols4[0:98, i:i + 1] for i in range(4)):
                sp.dma_start(win_dram[98 * n:98 * n + 98].rearrange("(n a) -> n a", a=1), c)\
                  .then_inc(G["win_stored"], 16)
            sp.wait_ge(G["win_stored"], 64)
            sp.dma_start(wide, win_dram.partition_broadcast(P)).then_inc(loads["win"], 16)

            def store_rows(s, width, tab):
                sp.sem_inc(s["lin_free"], 1)
                with sp.Fori(0, BI) as q:
                    sp.wait_ge(s["row"], (q + 1) * BU)
                    sp.dma_start(tab[bass.ds(q * (BU * P), BU * P), :].rearrange("(k p) f -> p k f", p=P),
                                 row_sb[:, :, 0:width]).then_inc(s["stored"], 16)
                    sp.wait_ge(s["stored"], (q + 1) * 16)
                    sp.sem_inc(s["lin_free"], 1)

            store_rows(s_in, ZW, z_tab)
            sp.wait_ge(G["top_ready"], 1)
            sp.dma_start(top_dram.rearrange("(n a) -> n a", a=1), top16[0:16, 0:1]).then_inc(G["top_stored"], 16)
            sp.wait_ge(G["top_stored"], 16)
            sp.dma_start(top_bc, top_dram.partition_broadcast(P)).then_inc(loads["top"], 16)

            sp.wait_ge(G["flags_ready"], 1)
            general = sp.value_load(flags_i[0:1, 1:2], min_val=0, max_val=1)
            with sp.If(general > 0):
                with sp.Fori(0, NG) as g:
                    sp.wait_ge(s_max["free"], g + 1)
                    sp.dma_start(idx[:, 0, :], src[bass.ds(g, 1), :, :].rearrange("a p t -> (a p) t"))\
                      .then_inc(s_max["idx"], 16)
                    sp.dma_start(dst_row.rearrange("a (t p) -> a t p", t=T),
                                 dst[bass.ds(g, 1), :, :].rearrange("a p t -> a t p"),
                                 allow_slow_non_contiguous=True).then_inc(s_max["dst"], 16)

            sp.wait_ge(G["er_ready_tab"], 1)
            sp.dma_start(er_tab[0:NB * P, :].rearrange("(k p) f -> p k f", p=P), erm).then_inc(G["er_stored"], 16)
            sp.dma_start(er_tab[NB * P:COLS, :], acc_b[:, 2, 0:2 * HEADS]).then_inc(G["er_stored"], 16)
            sp.wait_ge(G["er_stored"], 32)

            passes = sp.value_load(flags_i[0:1, 0:1], min_val=1, max_val=PASSES)
            with sp.Fori(0, passes) as k:
                hold(sp, G["pass_set"], k + 1)
                with sp.Fori(0, GI) as q:
                    n = sp.snap(k * GI + q, min_val=0, max_val=PASSES * GI)
                    for s in range(U):
                        sp.wait_ge(s_l1["rows_free"], n * U + (s + 1))
                        sp.dma_start(idx[:, s, :], src[bass.ds(q * U + s, 1), :, :].rearrange("a p t -> (a p) t"))\
                          .then_inc(s_l1["idx"][s], 16)
                        w0 = sp.value_load(win_i[0:1, bass.ds(q * U + s, 1)], min_val=0, max_val=COLS - WIN)
                        for half in range(2):
                            sp.dma_start(er_win[64 * half:64 * half + 64, s, 16 * half:16 * half + 16],
                                         er_tab[bass.ds(w0, WIN), :]).then_inc(s_l1["in"][s], 16)

            store_rows(s_mid, HIDDEN, up_tab)

            with sp.Fori(0, passes) as k:
                with sp.Fori(0, GI) as q:
                    n = sp.snap(k * GI + q, min_val=0, max_val=PASSES * GI)
                    for s in range(U):
                        sp.wait_ge(s_l2["rows_free"], n * U + (s + 1))
                        sp.dma_start(idx[:, s, :], src[bass.ds(q * U + s, 1), :, :].rearrange("a p t -> (a p) t"))\
                          .then_inc(s_l2["idx"][s], 16)
                        sp.dma_start(y_sb[:, s, :, :].rearrange("p t k -> p (t k)"),
                                     edge_y[bass.ds(q * U + s, 1), :, :].rearrange("a p t -> (a p) t"))\
                          .then_inc(s_l2["in"][s], 16)
                        sp.dma_start(ef_sb[:, s, :],
                                     edge_f[bass.ds(q * U + s, 1), :, :].rearrange("a p t -> (a p) t"))\
                          .then_inc(s_l2["in"][s], 16)

            for c in range(BI):
                sp.wait_ge(s_out["added"], BU * (c + 1))
                full = BU if c < BI - 1 else BU - 1
                sp.dma_start(out[c * BU * P:(c * BU + full) * P, :].rearrange("(k p) f -> p k f", p=P),
                             x_sb[:, c * BU:c * BU + full, :]).then_inc(s_out["stored"], 16)
            sp.dma_start(out[(NB - 1) * P:NODES, :], x_sb[0:TAIL, NB - 1, :]).then_inc(s_out["stored"], 16)
            sp.wait_ge(s_out["stored"], 16 * (BI + 1))

        @block.gpsimd
        def _(pool):
            for z in (a1_bd, a2_bd, a3_bd, wo_a, wo_b, w_up):
                pool.memset(z[:], 0.0).then_inc(zeroed, 1)
            pool.memset(er_win[:], 0.0).then_inc(zeroed, 1)
            pool.memset(acc_b[:], 0.0).then_inc(zeroed, 1)
            pool.memset(acc_a[:], 0.0).then_inc(zeroed, 1)

            def gather(s, table, width, done):
                for t in range(T):
                    pool.indirect_dma_start(out=rows[:, s, t, 0:width], out_offset=None, in_=table,
                                            in_offset=bass.IndirectOffsetOnAxis(ap=idx[:, s, t:t + 1], axis=0))\
                        .then_inc(done, 16)

            pool.wait_ge(s_in["stored"], 16 * BI)
            pool.wait_ge(G["flags_ready"], 1)
            general = pool.value_load(flags_i[0:1, 1:2], min_val=0, max_val=1)
            passes = pool.value_load(flags_i[0:1, 0:1], min_val=1, max_val=PASSES)
            with pool.If(general > 0):
                with pool.Fori(0, NG) as g:
                    hold(pool, s_max["idx"], (g + 1) * 16)
                    gather(0, z_tab, ZW, s_max["rows"])

            for s_l, tab, width, ready, count in ((s_l1, z_tab, ZW, s_in["stored"], 16 * BI),
                                                  (s_l2, up_tab, HIDDEN, s_mid["stored"], 16 * BI)):
                pool.wait_ge(ready, count)
                with pool.Fori(0, passes) as k:
                    with pool.Fori(0, GI) as q:
                        n = pool.snap(k * GI + q, min_val=0, max_val=PASSES * GI)
                        for s in range(U):
                            hold(pool, s_l["idx"][s], n * 16 + 16)
                            gather(s, tab, width, s_l["rows"][s])

        @block.scalar
        def _(act):
            def node_act(s, lin_cols):
                with act.Fori(0, BI) as q:
                    act.wait_ge(s["var"], q + 1)
                    nc.scalar.activation(std, mv[:, :, 1], ACT.Sqrt, bias=flags[:, 7:8]).then_inc(s["std"], 1)
                    act.wait_ge(s["stat"], q + 1)
                    for j in range(BU):
                        nc.scalar.activation(h_sb[:, j, :], x_sb[:, bass.ds(q * BU + j, 1), :].rearrange("p a f -> p (a f)"),
                                             ACT.Relu, bias=nmr[:, j:j + 1], scale=rstd[:, j:j + 1])\
                            .then_inc(s["norm"], 1)
                    act.wait_ge(s["turned"], (q + 1) * BU)
                    nc.scalar.activation(hT_sb[:, 0:4, :].rearrange("p a b -> p (a b)"), bank[0][:, :], ACT.Copy)
                    nc.scalar.activation(hT_sb[:, 4:7, :].rearrange("p a b -> p (a b)"), bank[1][:, 0:384], ACT.Copy)\
                        .then_inc(s["turned_sb"], 1)
                    act.wait_ge(s["lin"], (q + 1) * BU)
                    act.wait_ge(s["lin_free"], q + 1)
                    for b in range(3):
                        m = min(3, BU - 3 * b)
                        ins = nc.scalar.activation(row_sb[:, 3 * b:3 * b + m, 0:lin_cols],
                                                   bank[2 + b][:, 0:m * 144].rearrange("p (a b) -> p a b", b=144)
                                                   [:, :, 0:lin_cols], ACT.Copy)
                    if s is s_in:
                        ins.then_inc(step["act"], 1)
                        act.wait_ge(step["act"], q + 1)
                        nc.scalar.activation(elr[:, bass.ds(q * BU, BU), :], row_sb[:, :, HIDDEN:144], ACT.Copy)\
                            .then_inc(s["row"], BU)
                    else:
                        ins.then_inc(s["row"], BU)

            act.wait_ge(G["wT_ready"], 1)
            nc.scalar.activation(wT, bank[7][:, 0:P], ACT.Copy).then_inc(G["wT_copied"], 1)
            act.wait_ge(G["wa_ready"], 1)
            nc.scalar.activation(w_aug[:, HIDDEN:144], bank[7][:, 128:144], ACT.Copy).then_inc(G["w_ready"], 1)
            node_act(s_in, 144)

            act.wait_ge(G["flags_ready"], 1)
            passes = act.value_load(flags_i[0:1, 0:1], min_val=1, max_val=PASSES)
            with act.Fori(0, passes) as k:
                with act.Fori(0, GI) as q:
                    n = act.snap(k * GI + q, min_val=0, max_val=PASSES * GI)
                    for s in range(U):
                        h = s % 2
                        act.wait_ge(s_l1["turned"], n * U + (s + 1))
                        nc.scalar.activation(hotT[:, h, :], bank[0][:, :], ACT.Copy).then_inc(s_l1["hot_turned"], 1)
                        act.wait_ge(s_l1["score"], n * U + (s + 1))
                        nc.scalar.activation(a_sb[:, h, :, :].rearrange("p t h -> p (t h)"), e_sb[:, 3, :], ACT.Exp)\
                            .then_inc(s_l1["exp"], 1)

            with act.Fori(0, BI) as q:
                act.wait_ge(s_mid["agg_used"], q + 1)
                for j in range(BU):
                    nc.scalar.activation(h_sb[:, j, :], acc_a[:, bass.ds((q * BU + j) * P, P)], ACT.Copy)
                    nc.scalar.activation(hT_sb[0:HEADS, j, :], den_acc[:, bass.ds((q * BU + j) * P, P)], ACT.Copy)\
                        .then_inc(s_mid["agg_staged"], 1)
                act.wait_ge(s_mid["var"], q + 1)
                nc.scalar.activation(std, mv[:, :, 1], ACT.Sqrt, bias=flags[:, 7:8]).then_inc(s_mid["std"], 1)
                act.wait_ge(s_mid["stat"], q + 1)
                for j in range(BU):
                    nc.scalar.activation(h_sb[:, j, :], x_sb[:, bass.ds(q * BU + j, 1), :].rearrange("p a f -> p (a f)"),
                                         ACT.Relu, bias=nmr[:, j:j + 1], scale=rstd[:, j:j + 1])\
                        .then_inc(s_mid["norm"], 1)
                act.wait_ge(s_mid["turned"], (q + 1) * BU)
                nc.scalar.activation(hT_sb[:, 0:4, :].rearrange("p a b -> p (a b)"), bank[0][:, :], ACT.Copy)
                nc.scalar.activation(hT_sb[:, 4:7, :].rearrange("p a b -> p (a b)"), bank[1][:, 0:384], ACT.Copy)\
                    .then_inc(s_mid["turned_sb"], 1)
                act.wait_ge(s_mid["lin"], (q + 1) * BU)
                for b in range(3):
                    m = min(3, BU - 3 * b)
                    ins = nc.scalar.activation(row_sb[:, 3 * b:3 * b + m, 0:HIDDEN],
                                               bank[2 + b][:, 0:m * 144].rearrange("p (a b) -> p a b", b=144)
                                               [:, :, 0:HIDDEN], ACT.Copy)
                ins.then_inc(s_mid["row"], BU)

            with act.Fori(0, passes) as k:
                with act.Fori(0, GI) as q:
                    n = act.snap(k * GI + q, min_val=0, max_val=PASSES * GI)
                    for s in range(U):
                        act.wait_ge(s_l2["h1"], n * U + (s + 1))
                        nc.scalar.activation(h1_sb, bank[4][:, :], ACT.Silu, bias=vec[:, 2:3])\
                            .then_inc(s_l2["h1_act"], 1)
                        act.wait_ge(s_l2["h2"], n * U + (s + 1))
                        nc.scalar.activation(h2_sb[:, s % 2, :], bank[5][:, :], ACT.Silu, bias=vec[:, 3:4])\
                            .then_inc(s_l2["h2_act"], 1)

            with act.Fori(0, BI) as q:
                act.wait_ge(s_out["agg_used"], q * BU + 1)
                for j in range(BU):
                    at = (q * BU + j) * P
                    nc.scalar.activation(stage[:, j, 0, :], acc_a[:, bass.ds(at, P)], ACT.Copy)
                    nc.scalar.activation(stage[:, j, 1:4, :], acc_b[:, :, bass.ds(at, P)], ACT.Copy)\
                        .then_inc(s_out["agg_staged"], 1)

        @block.vector
        def _(dve):
            own = Own(dve, step["dve"])
            v = nc.vector

            v.memset(flags[:, 7:8], EPS)
            dve.wait_ge(loads["dst"], 16)
            own.after(v.tensor_copy(dst_rel[:, :, :], dst_i))
            own.after(v.tensor_reduce(redn[:, 0, :], dst_rel[:, :, :], AX.X, ALU.min))
            own.after(v.scalar_tensor_tensor(out=dst_i.bitcast(F32), in0=dst_rel[:, :, :], scalar=float(NODES),
                                             in1=dst_rel[:, :, :], op0=ALU.is_lt, op1=ALU.mult))
            v.tensor_reduce(redn[:, 1, :], dst_i.bitcast(F32), AX.X, ALU.max).then_inc(G["red_ready"], 1)
            dve.wait_ge(loads["attn"], 32)
            dve.wait_ge(loads["const"], 32)
            head = top_bc
            v.tensor_reduce(head[:, 0:HEADS], ident[:, :].rearrange("p (h q) -> p h q", q=PER_HEAD), AX.X, ALU.max)\
                .then_inc(G["attn_ready"], 1)
            dve.wait_ge(G["attn_ready"], 1)
            for n in range(2):
                v.tensor_scalar(attn_bd[:, 8 * n:8 * n + 8], head[:, 0:HEADS], vec[:, n:n + 1], None, ALU.mult)\
                    .then_inc(G["attn_ready"], 1)
            dve.wait_ge(G["red_turned"], 1)
            own.after(v.tensor_reduce(cols4[:, 0:2], bank[5][0:98, 0:256].rearrange("p (a b) -> p a b", b=P), AX.X,
                                      ALU.min))
            own.after(v.tensor_reduce(cols4[:, 2:4], bank[5][0:98, 256:512].rearrange("p (a b) -> p a b", b=P), AX.X,
                                      ALU.max))
            v.tensor_tensor(cols4[:, 2:4], cols4[:, 2:4], cols4[:, 0:2], ALU.subtract).then_inc(G["cols_ready"], 1)

            inv, inv2 = MUL ** -0.5, (2 * MUL) ** -0.5
            dve.wait_ge(loads["up"], 64)
            v.tensor_scalar(w_up[:, :], w_up[:, :], inv, None, ALU.mult).then_inc(G["up_w_ready"], 1)
            dve.wait_ge(loads["out_w"], 160)
            v.tensor_scalar(wo_a[:, :], wo_a[:, :], inv2 / 10.0, None, ALU.mult).then_inc(G["out_w_ready"], 1)
            v.tensor_scalar(wo_b[0:96, :, :], wo_b[0:96, :, :], inv2 / 10.0 / 3.0 ** 0.5, None, ALU.mult)\
                .then_inc(G["out_w_ready"], 1)
            v.tensor_scalar(wo_b[96:128, :, :], wo_b[96:128, :, :], inv2 / 10.0, None, ALU.mult)\
                .then_inc(G["out_w_ready"], 1)

            def norm_stats(s, q):
                for j in range(BU):
                    ins = v.bn_stats(stats[:, j, :], x_sb[:, bass.ds(q * BU + j, 1), :].rearrange("p a f -> p (a f)"))
                own_loop.after(ins, hold)
                for j in range(BU):
                    ins = v.bn_aggr(mv[:, j, :], stats[:, j, :])
                ins.then_inc(s["var"], 1)
                dve.wait_ge(s["std"], q + 1)
                own_loop.after(v.reciprocal(rstd, std))
                v.scalar_tensor_tensor(out=nmr, in0=mv[:, :, 0], scalar=-1.0, in1=rstd, op0=ALU.mult, op1=ALU.mult)\
                    .then_inc(s["stat"], 1)

            own_loop = Own(dve, sem("own_in"))
            dve.wait_ge(loads["x"], 16 * BI)
            with dve.Fori(0, BI) as q:
                own_loop.base, own_loop.n = q * 2, 0
                norm_stats(s_in, q)
                dve.wait_ge(s_in["norm"], (q + 1) * BU)
                assert own_loop.n == 2

            dve.wait_ge(s_in["row"], NB)
            ev = elr.rearrange("p k f -> p f k")
            own.after(v.tensor_reduce(top16[:, 0:8], ev[:, 0:8, :], AX.X, ALU.max))
            own.after(v.tensor_reduce(top16[:, 8:16], ev[:, 0:8, :], AX.X, ALU.min))
            v.tensor_scalar(top16[:, 8:16], top16[:, 8:16], -1.0, None, ALU.mult).then_inc(G["top_turned"], 1)
            dve.wait_ge(G["top_turned"], 2)
            v.tensor_reduce(top16[0:16, 0:1], bank[6][0:16, 0:P], AX.X, ALU.max).then_inc(G["top_ready"], 1)
            dve.wait_ge(loads["top"], 16)
            dve.wait_ge(loads["win"], 16)
            own.after(v.tensor_reduce(flags[:, 2:3], wide[:, NG:2 * NG], AX.X, ALU.max))
            own.after(v.tensor_scalar(flags[:, 0:1], flags[:, 2:3], WIN - 0.5, None, ALU.is_gt))
            own.after(v.tensor_tensor(flags[:, 3:4], top_bc[:, 0:1], top_bc[:, 8:9], ALU.add))
            for h in range(1, HEADS):
                own.after(v.tensor_tensor(flags[:, 4:5], top_bc[:, h:h + 1], top_bc[:, 8 + h:9 + h], ALU.add))
                own.after(v.tensor_tensor(flags[:, 3:4], flags[:, 3:4], flags[:, 4:5], ALU.max))
            own.after(v.tensor_scalar(flags[:, 1:2], flags[:, 3:4], SPREAD, None, ALU.is_le))
            own.after(v.tensor_scalar(flags[:, 1:2], flags[:, 1:2], -1.0, 1.0, ALU.mult, ALU.add))
            own.after(v.tensor_scalar(flags[:, 5:6], flags[:, 0:1], float(PASSES - 1), 1.0, ALU.mult, ALU.add))
            own.after(v.tensor_copy(flags_i[0:1, 0:1], flags[0:1, 5:6]))
            own.after(v.tensor_scalar(flags[:, 6:7], flags[:, 0:1], -1.0, 1.0, ALU.mult, ALU.add))
            own.after(v.tensor_scalar(wide[:, 0:NG], wide[:, 0:NG], flags[:, 6:7], None, ALU.mult))
            v.tensor_copy(flags_i[0:1, 1:2], flags[0:1, 1:2]).then_inc(G["flags_ready"], 1)
            own.after(v.tensor_copy(top, bc(top_bc[:, 0:HEADS], 1, NB)))

            def set_windows():
                own.after(v.tensor_copy(win_f[:, :], wide[:, 0:NG]))
                own.after(v.tensor_copy(win_i[0:1, :], win_f[0:1, :]))
                own.after(v.tensor_tensor(dst_rel[:, :, :], dst_rel[:, :, :],
                                          bc(win_f[:, :], 2, T),
                                          ALU.subtract))

            dve.wait_ge(G["flags_ready"], 1)
            general = dve.value_load(flags_i[0:1, 1:2], min_val=0, max_val=1)
            passes = dve.value_load(flags_i[0:1, 0:1], min_val=1, max_val=PASSES)
            dve.wait_ge(zeroed, 9)
            set_windows()
            with dve.If(general > 0):
                v.memset(max_acc, -3.0e38).then_inc(s_max["col"], 1)
                dve.sem_inc(s_max["free"], 1)
                with dve.Fori(0, NG) as g:
                    dve.wait_ge(s_max["turned"], g + 1)
                    for b in range(2):
                        ins = v.tensor_copy(elT_sb[:, 512 * b:512 * b + 512], bank[b][0:HEADS, :])
                    ins.then_inc(s_max["taken"], 1)
                    dve.wait_ge(s_max["taken"], g + 1)
                    hold(dve, s_max["dst"], g * 16 + 16)
                    with dve.Fori(0, GE) as e:
                        node = dve.value_load(dst_row[0:1, bass.ds(e, 1)], min_val=0, max_val=COLS - 1)
                        dve.wait_ge(s_max["col"], g * GE + e + 1)
                        v.tensor_tensor(max_acc[:, bass.ds(node, 1)], max_acc[:, bass.ds(node, 1)],
                                        elT_sb[:, bass.ds(e, 1)], ALU.max).then_inc(s_max["col"], 1)
                    dve.sem_inc(s_max["free"], 1)
                dve.wait_ge(s_max["col"], NG * GE + 1)
                with dve.Fori(0, NB) as b:
                    v.tensor_copy(stage_max, max_acc[:, bass.ds(b * P, P)]).then_inc(s_max["staged"], 1)
                    dve.wait_ge(s_max["blk"], b + 1)
                    v.tensor_copy(top[:, bass.ds(b, 1), :], bank[2][:, 0:HEADS].rearrange("p (a h) -> p a h", a=1))\
                        .then_inc(s_max["top"], 1)
                    dve.wait_ge(s_max["top"], b + 1)

            er_v = elr[:, :, 8:16]
            own.after(v.tensor_copy(erm[:, :, 0:8], er_v))
            own.after(v.tensor_tensor(top, top, er_v, ALU.add))
            v.scalar_tensor_tensor(out=erm[:, :, 8:16], in0=top, scalar=NEG_SLOPE, in1=top, op0=ALU.mult,
                                   op1=ALU.max).then_inc(G["er_ready_tab"], 1)
            dve.wait_ge(G["er_stored"], 32)

            def targets(q, s):
                return dst_rel[:, bass.ds(q * U + s, 1), :].rearrange("p a t -> p (a t)")

            def next_pass(dve):
                own_pass.after(v.tensor_scalar(win_f[:, :], win_f[:, :], float(WIN), None, ALU.add))
                own_pass.after(v.tensor_copy(win_i[0:1, :], win_f[0:1, :]))
                own_pass.after(v.tensor_scalar(dst_rel[:, :, :], dst_rel[:, :, :], -float(WIN), None, ALU.add))

            dve.sem_inc(s_l1["rows_free"], U)
            dve.sem_inc(s_l1["added"], 1)
            dve.sem_inc(G["pass_set"], 1)
            own_pass, own_l1 = Own(dve, sem("own_pass1")), Own(dve, sem("own_l1"))
            with dve.Fori(0, passes) as k:
                with dve.Fori(0, GI) as q:
                    n = dve.snap(k * GI + q, min_val=0, max_val=PASSES * GI)
                    own_l1.base, own_l1.n = n * (3 * U), 0

                    def add(s):
                        h = s % 2
                        w0 = dve.value_load(win_i[0:1, bass.ds(q * U + s, 1)], min_val=0, max_val=COLS - WIN)
                        dve.wait_ge(s_l1["agg"], n * U + (s + 1))
                        dve.wait_ge(s_l1["added"], n * U + (s + 1))
                        v.tensor_tensor(acc_a[:, bass.ds(w0, WIN)], acc_a[:, bass.ds(w0, WIN)],
                                        bank[2 + h][:, 0:WIN], ALU.add)
                        v.tensor_tensor(den_acc[:, bass.ds(w0, WIN)], den_acc[:, bass.ds(w0, WIN)],
                                        bank[4 + h][0:HEADS, 0:WIN], ALU.add).then_inc(s_l1["added"], 1)

                    for s in range(U):
                        h = s % 2
                        v.tensor_tensor(hot[:, h, :, :],
                                        bc(targets(q, s), 2, WIN),
                                        bc(iota[:, :], 1, T),
                                        ALU.is_equal).then_inc(s_l1["hot"], 1)
                        dve.wait_ge(s_l1["er"], n * U + (s + 1))
                        dve.wait_ge(s_l1["rows"][s], n * (16 * T) + 16 * T)
                        er_e = bank[1][:, 0:T * 16].rearrange("p (t f) -> p t f", f=16)
                        e3 = [e_sb[:, i, :].rearrange("p (t h) -> p t h", h=HEADS) for i in range(4)]
                        el_e = rows[:, s, :, HIDDEN:ZW]
                        own_l1.after(v.tensor_tensor(e3[0], el_e, er_e[:, :, 0:8], ALU.add))
                        own_l1.after(v.scalar_tensor_tensor(out=e3[1], in0=e3[0], scalar=NEG_SLOPE, in1=e3[0],
                                                            op0=ALU.mult, op1=ALU.max))
                        own_l1.after(v.tensor_tensor(e3[2], e3[1], er_e[:, :, 8:16], ALU.subtract))
                        v.tensor_scalar(e3[3], e3[2], 0.0, None, ALU.min).then_inc(s_l1["score"], 1)
                        dve.wait_ge(s_l1["exp"], n * U + (s + 1))
                        for hf in range(2):
                            ts = slice(hf * HT, hf * HT + HT)
                            ins = v.tensor_tensor(msg[:, h, ts, :].rearrange("p t (h f) -> p t h f", f=PER_HEAD),
                                                  rows[:, s, ts, 0:HIDDEN].rearrange("p t (h f) -> p t h f", f=PER_HEAD),
                                                  bc(a_sb[:, h, ts, :], 3, PER_HEAD), ALU.mult).then_inc(s_l1["msg"], 1)
                        dve.wait_ge(s_l1["msg"], (n * U + (s + 1)) * 2)
                        dve.sem_inc(s_l1["rows_free"], 1)
                        if s >= 1:
                            add(s - 1)
                    add(U - 1)
                    assert own_l1.n == 3 * U
                own_pass.base, own_pass.n = k * 3, 0
                next_pass(dve)
                dve.sem_inc(G["pass_set"], 1)

            dve.wait_ge(loads["bias"], 16)
            own_loop = Own(dve, sem("own_mid"))
            dve.wait_ge(s_l1["added"], passes * NG + 1)
            dve.sem_inc(s_mid["agg_used"], 1)
            with dve.Fori(0, BI) as q:
                own_loop.base, own_loop.n = q * 7, 0
                dve.wait_ge(s_mid["agg"], (q + 1) * BU)
                own_loop.after(v.tensor_scalar(rden, bank[7][:, 0:BU * HEADS], TINY, None, ALU.max))
                own_loop.after(v.reciprocal(rden, rden))
                xs = x_sb[:, bass.ds(q * BU, BU), :]
                own_loop.after(v.tensor_tensor(xs, xs, bc(bias_bc[:, :], 1, BU), ALU.add))
                rd = bc(rden.rearrange("p (t h) -> p t h", h=HEADS), 3, PER_HEAD)
                for b, (lo, hi) in enumerate(((0, 4), (4, 7))):
                    ins = v.tensor_tensor(row_sb[:, lo:hi, 0:HIDDEN].rearrange("p t (h f) -> p t h f", f=PER_HEAD),
                                          bank[5 + b][:, 0:(hi - lo) * P].rearrange("p (t h f) -> p t h f", h=HEADS,
                                                                                    f=PER_HEAD),
                                          rd[:, lo:hi, :, :], ALU.mult)
                own_loop.after(ins)
                own_loop.after(v.tensor_tensor(xs, xs, row_sb[:, :, 0:HIDDEN], ALU.add), hold)
                norm_stats(s_mid, q)
                dve.wait_ge(s_mid["stored"], q * 16 + 16)
                dve.sem_inc(s_mid["agg_used"], 1)
                assert own_loop.n == 7

            dve.wait_ge(s_mid["agg_staged"], NB)
            v.memset(acc_a[:, :], 0.0)
            v.memset(den_acc, 0.0)
            own.after(v.memset(max_acc, 0.0))
            own.after(v.tensor_tensor(dst_rel[:, :, :], dst_rel[:, :, :],
                                      bc(win_f[:, :], 2, T), ALU.add))
            set_windows()

            dve.sem_inc(s_l2["rows_free"], U)
            dve.sem_inc(s_l2["added"], 1)
            own_pass, own_l2 = Own(dve, sem("own_pass2")), Own(dve, sem("own_l2"))
            with dve.Fori(0, passes) as k:
                with dve.Fori(0, GI) as q:
                    n = dve.snap(k * GI + q, min_val=0, max_val=PASSES * GI)
                    own_l2.base, own_l2.n = n * (2 * U), 0

                    def add(s):
                        h = s % 2
                        w0 = dve.value_load(win_i[0:1, bass.ds(q * U + s, 1)], min_val=0, max_val=COLS - WIN)
                        dve.wait_ge(s_l2["half_free"], n * (2 * U) + (2 * s + 4))
                        dve.wait_ge(s_l2["added"], n * U + (s + 1))
                        v.tensor_tensor(acc_a[:, bass.ds(w0, WIN)], acc_a[:, bass.ds(w0, WIN)],
                                        bank[6 + h][:, 0:WIN], ALU.add)
                        v.tensor_tensor(acc_b[:, :, bass.ds(w0, WIN)], acc_b[:, :, bass.ds(w0, WIN)],
                                        bank[6 + h][:, WIN:4 * WIN].rearrange("p (k w) -> p k w", k=3), ALU.add)\
                            .then_inc(s_l2["added"], 1)

                    for s in range(U):
                        h = s % 2
                        dve.wait_ge(s_l2["in"][s], n * 32 + 32)
                        for hf in range(2):
                            ts = slice(hf * HT, hf * HT + HT)
                            own_l2.after(v.tensor_tensor(
                                eq[:, hf, :, :], bc(targets(q, s)[:, ts], 2, WIN),
                                bc(iota[:, :], 1, HT), ALU.is_equal))
                            dve.wait_ge(s_l2["half_free"], n * (2 * U) + (2 * s + hf + 1))
                            v.tensor_tensor(wy[:, hf, :, :].rearrange("p t (k w) -> p t k w", k=4),
                                            bc(eq[:, hf, :, :], 2, 4),
                                            bc(y_sb[:, s, ts, :], 3, WIN), ALU.mult)
                            if hf == 0:
                                dve.wait_ge(s_l2["tp"], n * U + (s + 1))
                                dve.wait_ge(s_l2["rows"][s], n * (16 * T) + 16 * T)
                            tp = [bank[2 * h + b][:, :].rearrange("p (j f m) -> p j f m", f=2, m=P)[:, :, hf, :]
                                  for b in range(2)]
                            for b in range(2):
                                t2 = slice(hf * HT + 2 * b, hf * HT + 2 * b + 2)
                                j2 = slice(2 * b, 2 * b + 2)
                                g_v = rows[:, s, t2, 0:96].rearrange("p t (i u) -> p t i u", u=MUL)
                                g_s = bc(rows[:, s, t2, 96:128], 2, 2)
                                for half, lo in ((0, 64), (1, 96)):
                                    v.tensor_tensor(prod[:, hf, j2, half, 0:96].rearrange("p t (i u) -> p t i u", u=MUL),
                                                    g_v, bc(tp[b][:, :, lo:lo + 32], 2, 3), ALU.mult)
                                ins = v.tensor_tensor(prod[:, hf, j2, :, 96:128], g_s,
                                                      tp[b][:, :, 0:64].rearrange("p t (i u) -> p t i u", u=MUL),
                                                      ALU.mult)
                            ins.then_inc(s_l2["prod"], 1)
                        dve.wait_ge(s_l2["prod"], n * (2 * U) + (2 * s + 2))
                        dve.sem_inc(s_l2["rows_free"], 1)
                        if s >= 1:
                            add(s - 1)
                    add(U - 1)
                    own_l2.n = 2 * U
                own_pass.base, own_pass.n = k * 3, 0
                next_pass(dve)

            dve.wait_ge(s_l2["added"], passes * NG + 1)
            dve.sem_inc(s_out["agg_used"], 1)
            with dve.Fori(0, BI) as q:
                for j in range(BU):
                    dve.wait_ge(s_out["agg"], q * BU + (j + 1))
                    xs = x_sb[:, bass.ds(q * BU + j, 1), :].rearrange("p a f -> p (a f)")
                    v.tensor_tensor(xs, xs, bank[j][:, 0:P], ALU.add).then_inc(s_out["added"], 1)
                dve.wait_ge(s_out["added"], (q + 1) * BU)
                dve.sem_inc(s_out["agg_used"], BU)

        @block.tensor
        def _(pe):
            t = nc.tensor
            pe.wait_ge(loads["const"], 32)
            pe.wait_ge(loads["w"], 16)
            t.transpose(bank[7][:, 0:P], w_aug[:, 0:HIDDEN], ident[:, :]).then_inc(G["wT_ready"], 1)
            pe.wait_ge(G["red_ready"], 1)
            for n in range(4):
                mm = t.transpose(bank[5][0:98, n * P:n * P + P], redn[:, n // 2, (n % 2) * 98:(n % 2) * 98 + 98],
                                 ident[:, :])
            mm.then_inc(G["red_turned"], 1)
            pe.wait_ge(G["attn_ready"], 3)
            pe.wait_ge(G["wT_copied"], 1)
            t.matmul(bank[7][:, 128:144], wT, attn_bd, start=True, stop=True).then_inc(G["wa_ready"], 1)
            pe.wait_ge(G["w_ready"], 1)

            def node_lin(s, q, weights, width):
                for j in range(BU):
                    pe.wait_ge(s["norm"], q * BU + (j + 1))
                    t.transpose(bank[j // 4][:, (j % 4) * P:(j % 4) * P + P], h_sb[:, j, :], ident[:, :])\
                        .then_inc(s["turned"], 1)
                pe.wait_ge(s["turned_sb"], q + 1)
                for j in range(BU):
                    t.matmul(bank[2 + j // 3][:, (j % 3) * 144:(j % 3) * 144 + width], hT_sb[:, j, :], weights,
                             start=True, stop=True).then_inc(s["lin"], 1)

            with pe.Fori(0, BI) as q:
                node_lin(s_in, q, w_aug[:, :], 144)

            pe.wait_ge(G["top_turned"], 1)
            t.transpose(bank[6][0:16, 0:P], top16, ident[:, :]).then_inc(G["top_turned"], 1)

            pe.wait_ge(G["flags_ready"], 1)
            general = pe.value_load(flags_i[0:1, 1:2], min_val=0, max_val=1)
            passes = pe.value_load(flags_i[0:1, 0:1], min_val=1, max_val=PASSES)
            with pe.If(general > 0):
                with pe.Fori(0, NG) as g:
                    pe.wait_ge(s_max["rows"], g * (16 * T) + 16 * T)
                    pe.wait_ge(s_max["free"], g + 1)
                    for i in range(T):
                        mm = t.transpose(bank[i // 4][0:HEADS, (i % 4) * P:(i % 4) * P + P],
                                         rows[:, 0, i, HIDDEN:ZW], ident[:, :])
                    mm.then_inc(s_max["turned"], 1)
                with pe.Fori(0, NB) as b:
                    hold(pe, s_max["staged"], b + 1)
                    t.transpose(bank[2][:, 0:HEADS], stage_max, ident[0:HEADS, 0:HEADS]).then_inc(s_max["blk"], 1)

            with pe.Fori(0, passes) as k:
                with pe.Fori(0, GI) as q:
                    n = pe.snap(k * GI + q, min_val=0, max_val=PASSES * GI)
                    for s in range(U):
                        h = s % 2
                        pe.wait_ge(s_l1["hot"], n * U + (s + 1))
                        for j in range(HT):
                            mm = t.transpose(bank[0][:, j * P:(j + 1) * P],
                                             hot[:, h, 2 * j:2 * j + 2, :].rearrange("p t w -> p (t w)"), ident[:, :])
                        mm.then_inc(s_l1["turned"], 1)
                        pe.wait_ge(s_l1["hot_turned"], n * U + (s + 1))
                        pe.wait_ge(s_l1["in"][s], n * 32 + 32)
                        for j in range(HT):
                            mm = t.matmul(bank[1][:, j * 32:j * 32 + 32], hotT[:, h, j * P:(j + 1) * P],
                                          er_win[:, s, :], start=True, stop=True)
                        mm.then_inc(s_l1["er"], 1)
                        for i in range(T):
                            if i % HT == 0:
                                pe.wait_ge(s_l1["msg"], (n * U + s) * 2 + (i // HT + 1))
                            t.matmul(bank[2 + h][:, 0:WIN], msg[:, h, i, :], hot[:, h, i, :],
                                     start=(i == 0), stop=(i == T - 1))
                            mm = t.matmul(bank[4 + h][0:HEADS, 0:WIN], a_sb[:, h, i, :], hot[:, h, i, :],
                                          start=(i == 0), stop=(i == T - 1))
                        mm.then_inc(s_l1["agg"], 1)

            pe.wait_ge(G["up_w_ready"], 1)
            with pe.Fori(0, BI) as q:
                for j in range(BU):
                    pe.wait_ge(s_mid["agg_staged"], q * BU + (j + 1))
                    t.transpose(bank[5 + j // 4][:, (j % 4) * P:(j % 4) * P + P], h_sb[:, j, :], ident[:, :])
                    t.transpose(bank[7][:, j * HEADS:(j + 1) * HEADS], hT_sb[0:HEADS, j, :], ident[0:HEADS, 0:HEADS])\
                        .then_inc(s_mid["agg"], 1)
                node_lin(s_mid, q, w_up[:, :], HIDDEN)

            pe.wait_ge(loads["mlp"], 160)
            pe.sem_inc(s_l2["half_free"], 2)
            with pe.Fori(0, passes) as k:
                with pe.Fori(0, GI) as q:
                    n = pe.snap(k * GI + q, min_val=0, max_val=PASSES * GI)

                    def radial(s):
                        h = s % 2
                        pe.wait_ge(s_l2["in"][s], n * 32 + 32)
                        t.matmul(bank[4][:, :], a1_bd[:, :], ef_sb[:, s, :], start=True, stop=True)\
                            .then_inc(s_l2["h1"], 1)
                        pe.wait_ge(s_l2["h1_act"], n * U + (s + 1))
                        t.matmul(bank[5][:, :], a2_bd[:, :], h1_sb, start=True, stop=True).then_inc(s_l2["h2"], 1)
                        pe.wait_ge(s_l2["h2_act"], n * U + (s + 1))
                        for j in range(HT):
                            mm = t.matmul(bank[2 * h + j // 2][:, (j % 2) * 256:(j % 2) * 256 + 256],
                                          h2_sb[:, h, j * P:(j + 1) * P], a3_bd[:, :], start=True, stop=True)
                        mm.then_inc(s_l2["tp"], 1)

                    def sums(s):
                        h = s % 2
                        for hf in range(2):
                            pe.wait_ge(s_l2["prod"], n * (2 * U) + (2 * s + hf + 1))
                            for j in range(HT):
                                st, en = (hf + j == 0), (hf == 1 and j == HT - 1)
                                t.matmul(bank[6 + h][:, 0:WIN], prod[:, hf, j, 0, :], wy[:, hf, j, 0:WIN],
                                         start=st, stop=en, skip_group_check=True)
                                mm = t.matmul(bank[6 + h][:, WIN:4 * WIN], prod[:, hf, j, 1, :],
                                              wy[:, hf, j, WIN:4 * WIN], start=False, stop=en, skip_group_check=True)
                            mm.then_inc(s_l2["half_free"], 1)

                    radial(0)
                    for s in range(U):
                        if s + 1 < U:
                            radial(s + 1)
                        sums(s)

            pe.wait_ge(G["out_w_ready"], 3)
            with pe.Fori(0, BI) as q:
                for j in range(BU):
                    pe.wait_ge(s_out["agg_staged"], q * BU + (j + 1))
                    for c in range(4):
                        mm = t.matmul(bank[j][:, 0:P], stage[:, j, c, :], wo_a[:, :] if c == 0 else wo_b[:, c - 1, :],
                                      start=(c == 0), stop=(c == 3))
                    mm.then_inc(s_out["agg"], 1)


def kernel(x, src, dst, edge_attr_4, edge_attr_8, **w):
    import numpy as np
    import concourse.bacc as bacc
    from concourse.bass_utils import run_bass_kernel_spmd

    extra = NG * GE - EDGES
    arrays = {
        "x": np.concatenate([np.asarray(x), np.zeros((NB * P - NODES, HIDDEN), np.float32)]),
        "src": np.concatenate([np.asarray(src), np.zeros(extra, np.int32)]).reshape(NG, P, T),
        "dst": np.concatenate([np.asarray(dst), np.full(extra, PAD_DST, np.int32)]).reshape(NG, P, T),
        "edge_y": np.concatenate([np.asarray(edge_attr_4), np.zeros((extra, 4), np.float32)]).reshape(NG, P, T * 4),
        "edge_f": np.ascontiguousarray(
            np.concatenate([np.asarray(edge_attr_8), np.zeros((extra, 8), np.float32)])
            .reshape(NG, P, 2, HT, 8).transpose(0, 2, 4, 3, 1)).reshape(NG, 16, HT * P),
    }
    for name, key in (("W", "L0_gnn_W"), ("attn_l", "L0_gnn_attn_l"), ("attn_r", "L0_gnn_attn_r"),
                      ("bias", "L0_gnn_bias"), ("W_up_s", "L1_gnn_W_up_s"), ("W_up_v", "L1_gnn_W_up_v"),
                      ("A1", "L1_gnn_A1"), ("b1", "L1_gnn_b1"), ("A2", "L1_gnn_A2"), ("b2", "L1_gnn_b2"),
                      ("A3", "L1_gnn_A3"), ("W_out_s", "L1_gnn_W_out_s"), ("W_out_v", "L1_gnn_W_out_v")):
        arrays[name] = np.ascontiguousarray(w[key])
    arrays["identity"] = np.concatenate([np.eye(P, dtype=np.float32),
                                         np.tile(np.arange(WIN + 2, dtype=np.float32), (P, 1))], axis=1)

    nc = bacc.Bacc("TRN2", target_bir_lowering=False, num_devices=1)
    args = [nc.dram_tensor(f"in_{n}", a.shape, mybir.dt.from_np(a.dtype), kind="ExternalInput").ap()
            for n, a in arrays.items()]
    out = nc.dram_tensor("out", (NODES, HIDDEN), F32, kind="ExternalOutput").ap()
    gnn_kernel(nc, *args, out)
    r = run_bass_kernel_spmd(nc, [{f"in_{n}": a for n, a in arrays.items()}], core_ids=[0])
    return r.results[0]["out"]
```

```python
from contextlib import ExitStack

import concourse.bass as bass
from concourse import mybir

F32 = mybir.dt.float32
I32 = mybir.dt.int32
ALU = mybir.AluOpType
ACT = mybir.ActivationFunctionType
AX = mybir.AxisListType

P = 128
NODES, EDGES, HIDDEN, HEADS, MUL = 6250, 200000, 128, 8, 32
PER_HEAD = HIDDEN // HEADS
NEG_SLOPE = 0.2
EPS = 1e-5

NB = -(-NODES // P)
BU = 7
BI = NB // BU
TAIL = NODES - (NB - 1) * P
COLS = (NB + 1) * P
PAD_DST = COLS - 1

T = 8
HT = T // 2
GE = T * P
NG = EDGES // GE + 1
U = 4
GI = NG // U
WIN = 48
PASSES = -(-NODES // WIN)
SPREAD = 80.0
TINY = 1e-36
ZW = HIDDEN + HEADS

assert NB == BU * BI and NG == U * GI and NG * GE >= EDGES and PAD_DST >= NODES + WIN


def bc(ap, axis, n):
    wide = ap.unsqueeze(axis)
    shape = list(wide.shape)
    shape[axis] = n
    return wide.broadcast_to(shape)


def gnn_kernel(nc, x, src, dst, edge_y, edge_f, W, attn_l, attn_r, bias, W_up_s, W_up_v, A1, b1, A2, b2, A3,
               W_out_s, W_out_v, identity, out):
    with ExitStack() as ctx:
        def sb(name, shape, dt=F32):
            return ctx.enter_context(nc.sbuf_tensor(name, shape, dt))

        def sem(name):
            return ctx.enter_context(nc.semaphore(name))

        def sems(name, n):
            return [sem(f"{name}{i}") for i in range(n)]

        def dram(name, shape, dt=F32):
            return nc.dram_tensor(name, shape, dt, kind="Internal").ap()

        z_tab = dram("z_tab", (NB * P, ZW))
        er_tab = dram("er_tab", (COLS, 2 * HEADS))
        up_tab = dram("up_tab", (NB * P, HIDDEN))
        win_dram = dram("win_dram", (2 * NG,))
        top_dram = dram("top_dram", (2 * HEADS,))

        pair = [ctx.enter_context(nc.psum_tensor(f"pair{i}", [P, 2, 512], F32)) for i in range(4)]
        bank = [pair[i // 2][:, i % 2, :] for i in range(8)]

        x_sb = sb("x_sb", [P, NB, HIDDEN])
        acc_a = sb("acc_a", [P, COLS])
        acc_b = sb("acc_b", [P, 3, COLS])
        den_acc = acc_b[0:HEADS, 0, :]
        max_acc = acc_b[0:HEADS, 1, :]
        dst_rel = sb("dst_rel", [P, NG, T])
        win_f = sb("win_f", [P, NG])
        win_i = sb("win_i", [1, NG], I32)
        ident = sb("ident", [P, P])
        iota = sb("iota", [P, WIN])
        flags = sb("flags", [P, 8])
        flags_i = sb("flags_i", [1, 2], I32)
        vec = sb("vec", [P, 8])
        bias_bc = sb("bias_bc", [P, HIDDEN])
        w_aug = sb("w_aug", [P, 144])
        w_up = sb("w_up", [P, HIDDEN])
        a1_bd = sb("a1_bd", [16, P])
        a2_bd = sb("a2_bd", [P, P])
        a3_bd = sb("a3_bd", [P, 2 * P])
        wo_a = sb("wo_a", [P, HIDDEN])
        wo_b = sb("wo_b", [P, 3, HIDDEN])
        rows = sb("rows", [P, U, T, ZW])
        idx = sb("idx", [P, U, T], I32)
        er_win = sb("er_win", [P, U, 4 * HEADS])
        y_sb = sb("y_sb", [P, U, T, 4])
        ef_sb = sb("ef_sb", [16, U, HT * P])

        share = sb("share", [P, 7424])

        def part(at, *shape, parts=P):
            n = 1
            for s in shape:
                n *= s
            flat = share[0:parts, at:at + n]
            names = "abcd"[:len(shape)]
            if len(shape) == 1:
                return flat
            return flat.rearrange(f"p ({' '.join(names)}) -> p {' '.join(names)}",
                                  **{c: s for c, s in zip(names[1:], shape[1:])})

        h_sb = part(0, BU, P)
        hT_sb = part(896, BU, P)
        row_sb = part(1792, BU, 144)
        stats = part(2800, BU, 6)
        mv = part(2842, BU, 2)
        mv_all = part(7168, NB, 2)
        std = part(7266, NB)
        rstd = part(7315, NB)
        nmr = part(7364, NB)
        rden = part(2877, BU * HEADS)
        elr = part(3000, NB, 2 * HEADS)
        erm = part(3784, NB, 2 * HEADS)
        top = part(4568, NB, HEADS)
        dst_i = part(4960, NG, T).bitcast(I32)
        redn = part(6528, 2, NG)
        wide = part(6528, 2 * NG)
        cols4 = part(6920, 4, parts=98)
        top16 = part(6924, 2 * HEADS)
        top_bc = part(6940, 2 * HEADS)
        wT = part(6960, P)
        attn_bd = part(7088, 2 * HEADS)
        stage_max = part(2048, P, parts=HEADS)
        elT_sb = part(0, GE, parts=HEADS)
        dst_row = part(1024, GE, parts=1).bitcast(I32)
        hot = part(0, U, T, WIN)
        hotT = part(1536, 2, 512)
        msg = part(2560, 2, T, P)
        e_sb = part(4608, 4, T * HEADS)
        a_sb = part(4864, 2, T, HEADS)
        eq = part(0, 2, HT, WIN)
        wy = part(512, 2, HT, 4 * WIN)
        prod = part(2560, 2, HT, 2, P)
        h1_sb = part(4608, 512)
        h2_sb = part(5120, 2, 512)
        stage = part(1792, BU, 4, P)

        loads = {n: sem(f"load_{n}") for n in
                 ("x", "const", "dst", "w", "attn", "bias", "mlp", "up", "out_w", "win", "top")}
        zeroed = sem("zeroed")
        step = {e: sem(f"own_{e}") for e in ("act", "dve")}
        wait_for = {n: sem(n) for n in (
            "red_ready", "red_turned", "cols_ready", "win_stored", "wT_ready", "wT_copied", "attn_ready", "wa_ready",
            "w_ready", "top_ready", "top_turned", "top_stored", "flags_ready", "er_stored", "er_ready_tab",
            "pass_set", "out_w_ready", "up_w_ready")}

        def node_sems(tag):
            return {n: sem(f"{tag}_{n}") for n in
                    ("var", "std", "stat", "norm", "turned", "turned_sb", "lin", "lin_free", "row", "stored",
                     "agg_staged", "agg", "agg_used", "added")}

        s_in, s_mid, s_out = node_sems("in"), node_sems("mid"), node_sems("out")

        def edge_sems(tag):
            one = {n: sem(f"{tag}_{n}") for n in
                   ("rows_free", "hot", "turned", "hot_turned", "er", "score", "exp", "msg", "agg", "added",
                    "h1", "h1_act", "h2", "h2_act", "tp", "prod", "half_free", "open")}
            one |= {n: sems(f"{tag}_{n}_slot", U) for n in ("idx", "rows", "in")}
            return one

        s_l1, s_l2 = edge_sems("l1"), edge_sems("l2")
        s_max = {n: sem(f"max_{n}") for n in ("idx", "rows", "dst", "free", "turned", "taken", "col", "staged", "blk",
                                              "top")}

        block = ctx.enter_context(nc.Block())
        G = wait_for

        passed = sem("passed")

        def plain_wait(eng, s, value):
            eng.wait_ge(s, value)

        def hold(eng, s, value):
            eng.wait_ge(s, value)
            eng.sem_inc(passed, 1)

        class Own:

            def __init__(self, eng, s):
                self.eng, self.s, self.n, self.base = eng, s, 0, None

            def after(self, ins, wait=None):
                ins.then_inc(self.s, 1)
                self.n += 1
                (wait or plain_wait)(self.eng, self.s, self.n if self.base is None else self.base + self.n)

        @block.sync
        def _(sp):
            sp.dma_start(dst_i, dst.rearrange("g p t -> p g t")).then_inc(loads["dst"], 16)
            sp.dma_start(ident[:, :], identity[:, 0:P]).then_inc(loads["const"], 16)
            sp.dma_start(iota[:, :], identity[:, P:P + WIN]).then_inc(loads["const"], 16)
            sp.dma_start(w_aug[:, 0:HIDDEN], W).then_inc(loads["w"], 16)
            for n, a in enumerate((attn_l, attn_r)):
                sp.dma_start(vec[:, n:n + 1], a.rearrange("h (p a) -> (h p) a", a=1)).then_inc(loads["attn"], 16)
            for c in range(BI):
                sp.dma_start(x_sb[:, c * BU:(c + 1) * BU, :],
                             x[c * BU * P:(c + 1) * BU * P, :].rearrange("(k p) f -> p k f", p=P))\
                  .then_inc(loads["x"], 16)
            sp.dma_start(bias_bc[:, :], bias.partition_broadcast(P)).then_inc(loads["bias"], 16)
            sp.wait_ge(zeroed, 7)
            for half in range(2):
                sp.dma_start(a1_bd[8 * half:8 * half + 8, 64 * half:64 * half + 64], A1).then_inc(loads["mlp"], 16)
                sp.dma_start(a2_bd[64 * half:64 * half + 64, 64 * half:64 * half + 64], A2).then_inc(loads["mlp"], 16)
                sp.dma_start(a3_bd[64 * half:64 * half + 64, P * half:P * half + P], A3).then_inc(loads["mlp"], 16)
                for n, b in enumerate((b1, b2)):
                    sp.dma_start(vec[64 * half:64 * half + 64, 2 + n:3 + n], b.rearrange("(n a) -> n a", a=1))\
                      .then_inc(loads["mlp"], 16)
            sp.dma_start(w_up[0:MUL, 96:128], W_up_s).then_inc(loads["up"], 16)
            sp.dma_start(wo_a[96:128, 0:MUL], W_out_s[0:MUL, :]).then_inc(loads["out_w"], 16)
            for i in range(3):
                sp.dma_start(w_up[MUL + i:P:3, MUL * i:MUL * i + MUL], W_up_v).then_inc(loads["up"], 16)
                vcols = wo_a[MUL * i:MUL * i + MUL, MUL + i:P:3]
                sp.dma_start(vcols, W_out_v[MUL:2 * MUL, :], allow_slow_non_contiguous=True).then_inc(loads["out_w"], 16)
                sp.dma_start(wo_b[MUL * i:MUL * i + MUL, i, 0:MUL], W_out_s[MUL:2 * MUL, :])\
                  .then_inc(loads["out_w"], 16)
                sp.dma_start(wo_b[96:128, i, MUL + i:P:3], W_out_v[0:MUL, :],
                             allow_slow_non_contiguous=True).then_inc(loads["out_w"], 16)

            sp.wait_ge(G["cols_ready"], 1)
            for n, c in enumerate(cols4[0:98, i:i + 1] for i in range(4)):
                sp.dma_start(win_dram[98 * n:98 * n + 98].rearrange("(n a) -> n a", a=1), c)\
                  .then_inc(G["win_stored"], 16)
            sp.wait_ge(G["win_stored"], 64)
            sp.dma_start(wide, win_dram.partition_broadcast(P)).then_inc(loads["win"], 16)

            def store_rows(s, width, tab):
                sp.sem_inc(s["lin_free"], 1)
                with sp.Fori(0, BI) as q:
                    sp.wait_ge(s["row"], q + 1)
                    sp.dma_start(tab[bass.ds(q * (BU * P), BU * P), :].rearrange("(k p) f -> p k f", p=P),
                                 row_sb[:, :, 0:width]).then_inc(s["stored"], 16)
                    sp.wait_ge(s["stored"], (q + 1) * 16)
                    sp.sem_inc(s["lin_free"], 1)

            store_rows(s_in, ZW, z_tab)
            sp.wait_ge(G["top_ready"], 1)
            sp.dma_start(top_dram.rearrange("(n a) -> n a", a=1), top16[0:16, 0:1]).then_inc(G["top_stored"], 16)
            sp.wait_ge(G["top_stored"], 16)
            sp.dma_start(top_bc, top_dram.partition_broadcast(P)).then_inc(loads["top"], 16)

            sp.wait_ge(G["flags_ready"], 1)
            general = sp.value_load(flags_i[0:1, 1:2], min_val=0, max_val=1)
            with sp.If(general > 0):
                with sp.Fori(0, NG) as g:
                    sp.wait_ge(s_max["free"], g + 1)
                    sp.dma_start(idx[:, 0, :], src[bass.ds(g, 1), :, :].rearrange("a p t -> (a p) t"))\
                      .then_inc(s_max["idx"], 16)
                    sp.dma_start(dst_row.rearrange("a (t p) -> a t p", t=T),
                                 dst[bass.ds(g, 1), :, :].rearrange("a p t -> a t p"),
                                 allow_slow_non_contiguous=True).then_inc(s_max["dst"], 16)

            sp.wait_ge(G["er_ready_tab"], 1)
            sp.dma_start(er_tab[0:NB * P, :].rearrange("(k p) f -> p k f", p=P), erm).then_inc(G["er_stored"], 16)
            sp.dma_start(er_tab[NB * P:COLS, :], acc_b[:, 2, 0:2 * HEADS]).then_inc(G["er_stored"], 16)
            sp.wait_ge(G["er_stored"], 32)

            passes = sp.value_load(flags_i[0:1, 0:1], min_val=1, max_val=PASSES)
            with sp.Fori(0, passes) as k:
                hold(sp, G["pass_set"], k + 1)
                with sp.Fori(0, GI) as q:
                    n = sp.snap(k * GI + q, min_val=0, max_val=PASSES * GI)
                    for s in range(U):
                        sp.wait_ge(s_l1["rows_free"], n * U + (s + 1))
                        sp.dma_start(idx[:, s, :], src[bass.ds(q * U + s, 1), :, :].rearrange("a p t -> (a p) t"))\
                          .then_inc(s_l1["idx"][s], 16)
                        w0 = sp.value_load(win_i[0:1, bass.ds(q * U + s, 1)], min_val=0, max_val=COLS - WIN)
                        for half in range(2):
                            sp.dma_start(er_win[WIN * half:WIN * half + WIN, s, 16 * half:16 * half + 16],
                                         er_tab[bass.ds(w0, WIN), :]).then_inc(s_l1["in"][s], 16)

            store_rows(s_mid, HIDDEN, up_tab)

            def load_edges(s, group):
                sp.dma_start(y_sb[:, s, :, :].rearrange("p t k -> p (t k)"),
                             edge_y[bass.ds(group, 1), :, :].rearrange("a p t -> (a p) t")).then_inc(s_l2["in"][s], 16)
                sp.dma_start(ef_sb[:, s, :], edge_f[bass.ds(group, 1), :, :].rearrange("a p t -> (a p) t"))\
                  .then_inc(s_l2["in"][s], 16)

            with sp.Fori(0, passes) as k:
                load_edges(0, 0)
                with sp.Fori(0, GI) as q:
                    n = sp.snap(k * GI + q, min_val=0, max_val=PASSES * GI)
                    for s in range(U):
                        i = n * U + s
                        sp.wait_ge(s_l2["rows_free"], i + 1)
                        sp.dma_start(idx[:, s, :], src[bass.ds(q * U + s, 1), :, :].rearrange("a p t -> (a p) t"))\
                          .then_inc(s_l2["idx"][s], 16)
                        hold(sp, s_l2["rows_free"], i + 2)
                        load_edges((s + 1) % U, q * U + (s + 1))
                hold(sp, s_l2["h1"], (k + 1) * (NG + 1))

            for c in range(BI):
                sp.wait_ge(s_out["added"], BU * (c + 2))
                full = BU if c < BI - 1 else BU - 1
                sp.dma_start(out[c * BU * P:(c * BU + full) * P, :].rearrange("(k p) f -> p k f", p=P),
                             x_sb[:, c * BU:c * BU + full, :]).then_inc(s_out["stored"], 16)
            sp.dma_start(out[(NB - 1) * P:NODES, :], x_sb[0:TAIL, NB - 1, :]).then_inc(s_out["stored"], 16)
            sp.wait_ge(s_out["stored"], 16 * (BI + 1))

        @block.gpsimd
        def _(pool):
            for z in (a1_bd, a2_bd, a3_bd, wo_a, wo_b, w_up):
                pool.memset(z[:], 0.0).then_inc(zeroed, 1)
            pool.memset(er_win[:], 0.0).then_inc(zeroed, 1)
            pool.memset(acc_b[:], 0.0).then_inc(zeroed, 1)
            pool.memset(acc_a[:], 0.0).then_inc(zeroed, 1)

            def gather(s, table, width, done):
                for t in range(T):
                    pool.indirect_dma_start(out=rows[:, s, t, 0:width], out_offset=None, in_=table,
                                            in_offset=bass.IndirectOffsetOnAxis(ap=idx[:, s, t:t + 1], axis=0))\
                        .then_inc(done, 16)

            pool.wait_ge(s_in["stored"], 16 * BI)
            pool.wait_ge(G["flags_ready"], 1)
            general = pool.value_load(flags_i[0:1, 1:2], min_val=0, max_val=1)
            passes = pool.value_load(flags_i[0:1, 0:1], min_val=1, max_val=PASSES)
            with pool.If(general > 0):
                with pool.Fori(0, NG) as g:
                    hold(pool, s_max["idx"], (g + 1) * 16)
                    gather(0, z_tab, ZW, s_max["rows"])

            for s_l, tab, width, ready, count in ((s_l1, z_tab, ZW, s_in["stored"], 16 * BI),
                                                  (s_l2, up_tab, HIDDEN, s_mid["stored"], 16 * BI)):
                pool.wait_ge(ready, count)
                with pool.Fori(0, passes) as k:
                    pool.sem_inc(s_l["open"], 1)
                    with pool.Fori(0, GI) as q:
                        n = pool.snap(k * GI + q, min_val=0, max_val=PASSES * GI)
                        for s in range(U):
                            hold(pool, s_l["idx"][s], n * 16 + 16)
                            gather(s, tab, width, s_l["rows"][s])
                    for s in range(U):
                        hold(pool, s_l["rows"][s], GI * 16 * T)
                    hold(pool, s_l["rows_free"], (k + 1) * NG + U)
                    pool.inc_swdge_sem(s_l["rows"], [GI * 16 * T] * U, mode="sub")

        @block.scalar
        def _(act):
            def node_norm(s):
                act.wait_ge(s["var"], 1)
                nc.scalar.activation(std, mv_all[:, :, 1], ACT.Sqrt, bias=flags[:, 7:8]).then_inc(s["std"], 1)
                act.wait_ge(s["stat"], 1)
                with act.Fori(0, BI) as q:
                    for j in range(BU):
                        act.wait_ge(s["turned"], q * BU + (j + 1))
                        at = bass.ds(q * BU + j, 1)
                        nc.scalar.activation(h_sb[:, j, :], x_sb[:, at, :].rearrange("p a f -> p (a f)"), ACT.Relu,
                                             bias=nmr[:, at], scale=rstd[:, at]).then_inc(s["norm"], 1)

            act.wait_ge(G["wT_ready"], 1)
            nc.scalar.activation(wT, bank[7][:, 0:P], ACT.Copy).then_inc(G["wT_copied"], 1)
            act.wait_ge(G["wa_ready"], 1)
            nc.scalar.activation(w_aug[:, HIDDEN:144], bank[7][:, 128:144], ACT.Copy).then_inc(G["w_ready"], 1)
            node_norm(s_in)

            act.wait_ge(G["flags_ready"], 1)
            passes = act.value_load(flags_i[0:1, 0:1], min_val=1, max_val=PASSES)
            with act.Fori(0, passes) as k:
                with act.Fori(0, GI) as q:
                    n = act.snap(k * GI + q, min_val=0, max_val=PASSES * GI)

                    def copy_turned(s):
                        act.wait_ge(s_l1["turned"], n * U + (s + 1))
                        nc.scalar.activation(hotT[0:2 * WIN, s % 2, :], bank[0][0:2 * WIN, :], ACT.Copy)\
                            .then_inc(s_l1["hot_turned"], 1)

                    copy_turned(0)
                    for s in range(U):
                        h = s % 2
                        act.wait_ge(s_l1["score"], n * U + (s + 1))
                        nc.scalar.activation(a_sb[:, h, :, :].rearrange("p t h -> p (t h)"), e_sb[:, 3, :], ACT.Exp)\
                            .then_inc(s_l1["exp"], 1)
                        if s + 1 < U:
                            copy_turned(s + 1)

            act.wait_ge(s_mid["agg_used"], 1)
            with act.Fori(0, BI) as q:
                for j in range(BU):
                    act.wait_ge(s_mid["agg"], q * BU + (j + 1))
                    nc.scalar.activation(h_sb[:, j, :], acc_a[:, bass.ds((q * BU + j) * P, P)], ACT.Copy)
                    nc.scalar.activation(hT_sb[0:HEADS, j, :], den_acc[:, bass.ds((q * BU + j) * P, P)], ACT.Copy)\
                        .then_inc(s_mid["agg_staged"], 1)
            node_norm(s_mid)

            def hidden(m, h):
                act.wait_ge(s_l2["h1"], m + 1)
                nc.scalar.activation(h1_sb, bank[4], ACT.Silu, bias=vec[:, 2:3]).then_inc(s_l2["h1_act"], 1)
                act.wait_ge(s_l2["h2"], m + 1)
                nc.scalar.activation(h2_sb[:, h, :], bank[5], ACT.Silu, bias=vec[:, 3:4]).then_inc(s_l2["h2_act"], 1)

            with act.Fori(0, passes) as k:
                hidden(k * (NG + 1), 0)
                with act.Fori(0, GI) as q:
                    n = act.snap(k * (NG + 1) + q * U, min_val=0, max_val=PASSES * (NG + 1))
                    for s in range(U):
                        hidden(n + (s + 1), (s + 1) % 2)

            act.wait_ge(s_out["agg_used"], 1)
            with act.Fori(0, BI) as q:
                for j in range(BU):
                    act.wait_ge(s_out["agg"], q * BU + (j + 1))
                    nc.scalar.activation(stage[:, j, 1:4, :], acc_b[:, :, bass.ds((q * BU + j) * P, P)], ACT.Copy)\
                        .then_inc(s_out["agg_staged"], 1)

        @block.vector
        def _(dve):
            own = Own(dve, step["dve"])
            v = nc.vector

            v.memset(flags[:, 7:8], EPS)
            dve.wait_ge(loads["dst"], 16)
            own.after(v.tensor_copy(dst_rel[:, :, :], dst_i))
            own.after(v.tensor_reduce(redn[:, 0, :], dst_rel[:, :, :], AX.X, ALU.min))
            own.after(v.scalar_tensor_tensor(out=dst_i.bitcast(F32), in0=dst_rel[:, :, :], scalar=float(NODES),
                                             in1=dst_rel[:, :, :], op0=ALU.is_lt, op1=ALU.mult))
            v.tensor_reduce(redn[:, 1, :], dst_i.bitcast(F32), AX.X, ALU.max).then_inc(G["red_ready"], 1)
            dve.wait_ge(loads["attn"], 32)
            dve.wait_ge(loads["const"], 32)
            head = top_bc
            v.tensor_reduce(head[:, 0:HEADS], ident[:, :].rearrange("p (h q) -> p h q", q=PER_HEAD), AX.X, ALU.max)\
                .then_inc(G["attn_ready"], 1)
            dve.wait_ge(G["attn_ready"], 1)
            for n in range(2):
                v.tensor_scalar(attn_bd[:, 8 * n:8 * n + 8], head[:, 0:HEADS], vec[:, n:n + 1], None, ALU.mult)\
                    .then_inc(G["attn_ready"], 1)
            dve.wait_ge(G["red_turned"], 1)
            own.after(v.tensor_reduce(cols4[:, 0:2], bank[5][0:98, 0:256].rearrange("p (a b) -> p a b", b=P), AX.X,
                                      ALU.min))
            own.after(v.tensor_reduce(cols4[:, 2:4], bank[5][0:98, 256:512].rearrange("p (a b) -> p a b", b=P), AX.X,
                                      ALU.max))
            v.tensor_tensor(cols4[:, 2:4], cols4[:, 2:4], cols4[:, 0:2], ALU.subtract).then_inc(G["cols_ready"], 1)

            inv, inv2 = MUL ** -0.5, (2 * MUL) ** -0.5
            dve.wait_ge(loads["up"], 64)
            v.tensor_scalar(w_up[:, :], w_up[:, :], inv, None, ALU.mult).then_inc(G["up_w_ready"], 1)
            dve.wait_ge(loads["out_w"], 160)
            v.tensor_scalar(wo_a[:, :], wo_a[:, :], inv2 / 10.0, None, ALU.mult).then_inc(G["out_w_ready"], 1)
            v.tensor_scalar(wo_b[0:96, :, :], wo_b[0:96, :, :], inv2 / 10.0 / 3.0 ** 0.5, None, ALU.mult)\
                .then_inc(G["out_w_ready"], 1)
            v.tensor_scalar(wo_b[96:128, :, :], wo_b[96:128, :, :], inv2 / 10.0, None, ALU.mult)\
                .then_inc(G["out_w_ready"], 1)

            def norm_stats(q):
                for j in range(BU):
                    ins = v.bn_stats(stats[:, j, :], x_sb[:, bass.ds(q * BU + j, 1), :].rearrange("p a f -> p (a f)"))
                own_loop.after(ins, hold)
                for j in range(BU):
                    ins = v.bn_aggr(mv[:, j, :], stats[:, j, :])
                own_loop.after(ins)
                own_loop.after(v.tensor_copy(mv_all[:, bass.ds(q * BU, BU), :], mv), hold)

            def norm_scale(s):
                dve.sem_inc(s["var"], 1)
                dve.wait_ge(s["std"], 1)
                own.after(v.reciprocal(rstd, std))
                v.scalar_tensor_tensor(out=nmr, in0=mv_all[:, :, 0], scalar=-1.0, in1=rstd, op0=ALU.mult,
                                       op1=ALU.mult).then_inc(s["stat"], 1)

            def node_rows(s, width):
                with dve.Fori(0, BI) as q:
                    dve.wait_ge(s["turned"], (q + 2) * BU)
                    v.tensor_copy(hT_sb[:, 0:4, :].rearrange("p a b -> p (a b)"), bank[0])
                    v.tensor_copy(hT_sb[:, 4:7, :].rearrange("p a b -> p (a b)"), bank[1][:, 0:384])\
                        .then_inc(s["turned_sb"], 1)
                    dve.wait_ge(s["lin"], q + 1)
                    dve.wait_ge(s["lin_free"], q + 1)
                    for b in range(3):
                        m = min(3, BU - 3 * b)
                        lin = bank[2 + b][:, 0:m * 144].rearrange("p (a b) -> p a b", b=144)
                        if s is s_in:
                            v.tensor_copy(elr[:, bass.ds(q * BU + 3 * b, m), :], lin[:, :, HIDDEN:144])
                        ins = v.tensor_copy(row_sb[:, 3 * b:3 * b + m, 0:width], lin[:, :, 0:width])
                    ins.then_inc(s["row"], 1)

            own_loop = Own(dve, sem("own_in"))
            dve.wait_ge(loads["x"], 16 * BI)
            with dve.Fori(0, BI) as q:
                own_loop.base, own_loop.n = q * 3, 0
                norm_stats(q)
                assert own_loop.n == 3
            norm_scale(s_in)
            node_rows(s_in, ZW)

            dve.wait_ge(s_in["row"], BI)
            ev = elr.rearrange("p k f -> p f k")
            own.after(v.tensor_reduce(top16[:, 0:8], ev[:, 0:8, :], AX.X, ALU.max))
            own.after(v.tensor_reduce(top16[:, 8:16], ev[:, 0:8, :], AX.X, ALU.min))
            v.tensor_scalar(top16[:, 8:16], top16[:, 8:16], -1.0, None, ALU.mult).then_inc(G["top_turned"], 1)
            dve.wait_ge(G["top_turned"], 2)
            v.tensor_reduce(top16[0:16, 0:1], bank[6][0:16, 0:P], AX.X, ALU.max).then_inc(G["top_ready"], 1)
            dve.wait_ge(loads["top"], 16)
            dve.wait_ge(loads["win"], 16)
            own.after(v.tensor_reduce(flags[:, 2:3], wide[:, NG:2 * NG], AX.X, ALU.max))
            own.after(v.tensor_scalar(flags[:, 0:1], flags[:, 2:3], WIN - 0.5, None, ALU.is_gt))
            own.after(v.tensor_tensor(flags[:, 3:4], top_bc[:, 0:1], top_bc[:, 8:9], ALU.add))
            for h in range(1, HEADS):
                own.after(v.tensor_tensor(flags[:, 4:5], top_bc[:, h:h + 1], top_bc[:, 8 + h:9 + h], ALU.add))
                own.after(v.tensor_tensor(flags[:, 3:4], flags[:, 3:4], flags[:, 4:5], ALU.max))
            own.after(v.tensor_scalar(flags[:, 1:2], flags[:, 3:4], SPREAD, None, ALU.is_le))
            own.after(v.tensor_scalar(flags[:, 1:2], flags[:, 1:2], -1.0, 1.0, ALU.mult, ALU.add))
            own.after(v.tensor_scalar(flags[:, 5:6], flags[:, 0:1], float(PASSES - 1), 1.0, ALU.mult, ALU.add))
            own.after(v.tensor_copy(flags_i[0:1, 0:1], flags[0:1, 5:6]))
            own.after(v.tensor_scalar(flags[:, 6:7], flags[:, 0:1], -1.0, 1.0, ALU.mult, ALU.add))
            own.after(v.tensor_scalar(wide[:, 0:NG], wide[:, 0:NG], flags[:, 6:7], None, ALU.mult))
            v.tensor_copy(flags_i[0:1, 1:2], flags[0:1, 1:2]).then_inc(G["flags_ready"], 1)
            own.after(v.tensor_copy(top, bc(top_bc[:, 0:HEADS], 1, NB)))

            def set_windows():
                own.after(v.tensor_copy(win_f[:, :], wide[:, 0:NG]))
                own.after(v.tensor_copy(win_i[0:1, :], win_f[0:1, :]))
                own.after(v.tensor_tensor(dst_rel[:, :, :], dst_rel[:, :, :],
                                          bc(win_f[:, :], 2, T),
                                          ALU.subtract))

            dve.wait_ge(G["flags_ready"], 1)
            general = dve.value_load(flags_i[0:1, 1:2], min_val=0, max_val=1)
            passes = dve.value_load(flags_i[0:1, 0:1], min_val=1, max_val=PASSES)
            dve.wait_ge(zeroed, 9)
            set_windows()
            with dve.If(general > 0):
                v.memset(max_acc, -3.0e38).then_inc(s_max["col"], 1)
                dve.sem_inc(s_max["free"], 1)
                with dve.Fori(0, NG) as g:
                    dve.wait_ge(s_max["turned"], g + 1)
                    for b in range(2):
                        ins = v.tensor_copy(elT_sb[:, 512 * b:512 * b + 512], bank[b][0:HEADS, :])
                    ins.then_inc(s_max["taken"], 1)
                    dve.wait_ge(s_max["taken"], g + 1)
                    hold(dve, s_max["dst"], g * 16 + 16)
                    with dve.Fori(0, GE) as e:
                        node = dve.value_load(dst_row[0:1, bass.ds(e, 1)], min_val=0, max_val=COLS - 1)
                        dve.wait_ge(s_max["col"], g * GE + e + 1)
                        v.tensor_tensor(max_acc[:, bass.ds(node, 1)], max_acc[:, bass.ds(node, 1)],
                                        elT_sb[:, bass.ds(e, 1)], ALU.max).then_inc(s_max["col"], 1)
                    dve.wait_ge(s_max["col"], (g + 1) * GE + 1)
                    dve.sem_inc(s_max["free"], 1)
                dve.wait_ge(s_max["col"], NG * GE + 1)
                with dve.Fori(0, NB) as b:
                    v.tensor_copy(stage_max, max_acc[:, bass.ds(b * P, P)]).then_inc(s_max["staged"], 1)
                    dve.wait_ge(s_max["blk"], b + 1)
                    v.tensor_copy(top[:, bass.ds(b, 1), :], bank[2][:, 0:HEADS].rearrange("p (a h) -> p a h", a=1))\
                        .then_inc(s_max["top"], 1)
                    dve.wait_ge(s_max["top"], b + 1)

            er_v = elr[:, :, 8:16]
            own.after(v.tensor_copy(erm[:, :, 0:8], er_v))
            own.after(v.tensor_tensor(top, top, er_v, ALU.add))
            v.scalar_tensor_tensor(out=erm[:, :, 8:16], in0=top, scalar=NEG_SLOPE, in1=top, op0=ALU.mult,
                                   op1=ALU.max).then_inc(G["er_ready_tab"], 1)
            dve.wait_ge(G["er_stored"], 32)

            def targets(q, s):
                return dst_rel[:, bass.ds(q * U + s, 1), :].rearrange("p a t -> p (a t)")

            def next_pass(dve):
                own_pass.after(v.tensor_scalar(win_f[:, :], win_f[:, :], float(WIN), None, ALU.add))
                own_pass.after(v.tensor_copy(win_i[0:1, :], win_f[0:1, :]))
                own_pass.after(v.tensor_scalar(dst_rel[:, :, :], dst_rel[:, :, :], -float(WIN), None, ALU.add))

            dve.sem_inc(s_l1["rows_free"], U)
            dve.sem_inc(s_l1["added"], 1)
            dve.sem_inc(G["pass_set"], 1)
            own_pass, own_l1 = Own(dve, sem("own_pass1")), Own(dve, sem("own_l1"))
            with dve.Fori(0, passes) as k:
                hold(dve, s_l1["open"], k + 1)
                with dve.Fori(0, GI) as q:
                    n = dve.snap(k * GI + q, min_val=0, max_val=PASSES * GI)
                    own_l1.base, own_l1.n = n * (3 * U), 0

                    def add(s):
                        h = s % 2
                        w0 = dve.value_load(win_i[0:1, bass.ds(q * U + s, 1)], min_val=0, max_val=COLS - WIN)
                        dve.wait_ge(s_l1["agg"], n * U + (s + 1))
                        dve.wait_ge(s_l1["added"], n * U + (s + 1))
                        v.tensor_tensor(acc_a[:, bass.ds(w0, WIN)], acc_a[:, bass.ds(w0, WIN)],
                                        bank[2 + h][:, 0:WIN], ALU.add)
                        v.tensor_tensor(den_acc[:, bass.ds(w0, WIN)], den_acc[:, bass.ds(w0, WIN)],
                                        bank[4 + h][0:HEADS, 0:WIN], ALU.add).then_inc(s_l1["added"], 1)

                    def one_hot(s):
                        v.tensor_tensor(hot[:, s, :, :], bc(targets(q, s), 2, WIN), bc(iota[:, :], 1, T),
                                        ALU.is_equal).then_inc(s_l1["hot"], 1)

                    one_hot(0)
                    for s in range(U):
                        h = s % 2
                        dve.wait_ge(s_l1["er"], n * U + (s + 1))
                        dve.wait_ge(s_l1["rows"][s], q * (16 * T) + 16 * T)
                        er_e = bank[6 + h][:, 0:T * 16].rearrange("p (t f) -> p t f", f=16)
                        e3 = [e_sb[:, i, :].rearrange("p (t h) -> p t h", h=HEADS) for i in range(4)]
                        el_e = rows[:, s, :, HIDDEN:ZW]
                        own_l1.after(v.tensor_tensor(e3[0], el_e, er_e[:, :, 0:8], ALU.add))
                        own_l1.after(v.scalar_tensor_tensor(out=e3[1], in0=e3[0], scalar=NEG_SLOPE, in1=e3[0],
                                                            op0=ALU.mult, op1=ALU.max))
                        own_l1.after(v.tensor_tensor(e3[2], e3[1], er_e[:, :, 8:16], ALU.subtract))
                        v.tensor_scalar(e3[3], e3[2], 0.0, None, ALU.min).then_inc(s_l1["score"], 1)
                        if s + 1 < U:
                            one_hot(s + 1)
                        dve.wait_ge(s_l1["exp"], n * U + (s + 1))
                        for hf in range(2):
                            ts = slice(hf * HT, hf * HT + HT)
                            ins = v.tensor_tensor(msg[:, h, ts, :].rearrange("p t (h f) -> p t h f", f=PER_HEAD),
                                                  rows[:, s, ts, 0:HIDDEN].rearrange("p t (h f) -> p t h f", f=PER_HEAD),
                                                  bc(a_sb[:, h, ts, :], 3, PER_HEAD), ALU.mult).then_inc(s_l1["msg"], 1)
                        dve.wait_ge(s_l1["msg"], (n * U + (s + 1)) * 2)
                        dve.sem_inc(s_l1["rows_free"], 1)
                        if s >= 1:
                            add(s - 1)
                    add(U - 1)
                    assert own_l1.n == 3 * U
                own_pass.base, own_pass.n = k * 3, 0
                next_pass(dve)
                dve.sem_inc(G["pass_set"], 1)

            dve.wait_ge(loads["bias"], 16)
            own_loop = Own(dve, sem("own_mid"))
            dve.wait_ge(s_l1["added"], passes * NG + 1)
            dve.sem_inc(s_mid["agg_used"], 1)
            with dve.Fori(0, BI) as q:
                own_loop.base, own_loop.n = q * 8, 0
                dve.wait_ge(s_mid["agg"], (q + 2) * BU)
                own_loop.after(v.tensor_scalar(rden, bank[7][:, 0:BU * HEADS], TINY, None, ALU.max))
                own_loop.after(v.reciprocal(rden, rden))
                rd = bc(rden.rearrange("p (t h) -> p t h", h=HEADS), 3, PER_HEAD)
                for b, (lo, hi) in enumerate(((0, 4), (4, 7))):
                    ins = v.tensor_tensor(row_sb[:, lo:hi, 0:HIDDEN].rearrange("p t (h f) -> p t h f", f=PER_HEAD),
                                          bank[5 + b][:, 0:(hi - lo) * P].rearrange("p (t h f) -> p t h f", h=HEADS,
                                                                                    f=PER_HEAD),
                                          rd[:, lo:hi, :, :], ALU.mult)
                own_loop.after(ins)
                dve.sem_inc(s_mid["agg_used"], 1)
                xs = x_sb[:, bass.ds(q * BU, BU), :]
                own_loop.after(v.tensor_tensor(xs, xs, bc(bias_bc[:, :], 1, BU), ALU.add))
                own_loop.after(v.tensor_tensor(xs, xs, row_sb[:, :, 0:HIDDEN], ALU.add), hold)
                norm_stats(q)
                assert own_loop.n == 8
            norm_scale(s_mid)

            dve.wait_ge(s_mid["agg_staged"], NB)
            v.memset(acc_a[:, :], 0.0)
            v.memset(den_acc, 0.0)
            own.after(v.memset(max_acc, 0.0))
            node_rows(s_mid, HIDDEN)

            own.after(v.tensor_tensor(dst_rel[:, :, :], dst_rel[:, :, :],
                                      bc(win_f[:, :], 2, T), ALU.add))
            set_windows()

            dve.sem_inc(s_l2["rows_free"], U)
            dve.sem_inc(s_l2["added"], 1)
            own_pass, own_l2 = Own(dve, sem("own_pass2")), Own(dve, sem("own_l2"))
            with dve.Fori(0, passes) as k:
                hold(dve, s_l2["open"], k + 1)
                with dve.Fori(0, GI) as q:
                    n = dve.snap(k * GI + q, min_val=0, max_val=PASSES * GI)
                    own_l2.base, own_l2.n = n * (2 * U), 0

                    def add(s):
                        h = s % 2
                        w0 = dve.value_load(win_i[0:1, bass.ds(q * U + s, 1)], min_val=0, max_val=COLS - WIN)
                        dve.wait_ge(s_l2["half_free"], n * (2 * U) + (2 * s + 4))
                        dve.wait_ge(s_l2["added"], n * U + (s + 1))
                        v.tensor_tensor(acc_a[:, bass.ds(w0, WIN)], acc_a[:, bass.ds(w0, WIN)],
                                        bank[6 + h][:, 0:WIN], ALU.add)
                        v.tensor_tensor(acc_b[:, :, bass.ds(w0, WIN)], acc_b[:, :, bass.ds(w0, WIN)],
                                        bank[6 + h][:, WIN:4 * WIN].rearrange("p (k w) -> p k w", k=3), ALU.add)\
                            .then_inc(s_l2["added"], 1)

                    for s in range(U):
                        h = s % 2
                        dve.wait_ge(s_l2["in"][s], (n + k) * 32 + 32 if s == 0 else n * 32 + 32)
                        for hf in range(2):
                            ts = slice(hf * HT, hf * HT + HT)
                            own_l2.after(v.tensor_tensor(
                                eq[:, hf, :, :], bc(targets(q, s)[:, ts], 2, WIN),
                                bc(iota[:, :], 1, HT), ALU.is_equal))
                            dve.wait_ge(s_l2["half_free"], n * (2 * U) + (2 * s + hf + 1))
                            v.tensor_tensor(wy[:, hf, :, :].rearrange("p t (k w) -> p t k w", k=4),
                                            bc(eq[:, hf, :, :], 2, 4),
                                            bc(y_sb[:, s, ts, :], 3, WIN), ALU.mult)
                            if hf == 0:
                                dve.wait_ge(s_l2["tp"], n * U + k + (s + 1))
                                dve.wait_ge(s_l2["rows"][s], q * (16 * T) + 16 * T)
                            tp = pair[h][:, :, :].rearrange("p b (j f m) -> p (b j) f m", f=2, m=P)[:, :, hf, :]
                            g_v = rows[:, s, ts, 0:96].rearrange("p t (i u) -> p t i u", u=MUL)
                            for half, lo in ((0, 64), (1, 96)):
                                v.tensor_tensor(prod[:, hf, :, half, 0:96].rearrange("p t (i u) -> p t i u", u=MUL),
                                                g_v, bc(tp[:, :, lo:lo + 32], 2, 3), ALU.mult)
                            ins = v.tensor_tensor(prod[:, hf, :, :, 96:128], bc(rows[:, s, ts, 96:128], 2, 2),
                                                  tp[:, :, 0:64].rearrange("p t (i u) -> p t i u", u=MUL), ALU.mult)
                            ins.then_inc(s_l2["prod"], 1)
                        dve.wait_ge(s_l2["prod"], n * (2 * U) + (2 * s + 2))
                        dve.sem_inc(s_l2["rows_free"], 1)
                        if s >= 1:
                            add(s - 1)
                    add(U - 1)
                    own_l2.n = 2 * U
                own_pass.base, own_pass.n = k * 3, 0
                next_pass(dve)

            dve.wait_ge(s_l2["added"], passes * NG + 1)
            dve.wait_ge(s_l2["tp"], passes * (NG + 1))
            dve.sem_inc(s_out["agg_used"], 1)
            with dve.Fori(0, BI) as q:
                for j in range(BU):
                    dve.wait_ge(s_out["agg"], q * BU + (j + 1))
                    v.tensor_copy(stage[:, j, 0, :], acc_a[:, bass.ds((q * BU + j) * P, P)])\
                        .then_inc(s_out["turned_sb"], 1)
                for j in range(BU):
                    dve.wait_ge(s_out["agg"], (q + 1) * BU + (j + 1))
                    xs = x_sb[:, bass.ds(q * BU + j, 1), :].rearrange("p a f -> p (a f)")
                    v.tensor_tensor(xs, xs, bank[j][:, 0:P], ALU.add).then_inc(s_out["added"], 1)

        @block.tensor
        def _(pe):
            t = nc.tensor
            pe.wait_ge(loads["const"], 32)
            pe.wait_ge(loads["w"], 16)
            t.transpose(bank[7][:, 0:P], w_aug[:, 0:HIDDEN], ident[:, :]).then_inc(G["wT_ready"], 1)
            pe.wait_ge(G["red_ready"], 1)
            for n in range(4):
                mm = t.transpose(bank[5][0:98, n * P:n * P + P], redn[:, n // 2, (n % 2) * 98:(n % 2) * 98 + 98],
                                 ident[:, :])
            mm.then_inc(G["red_turned"], 1)
            pe.wait_ge(G["attn_ready"], 3)
            pe.wait_ge(G["wT_copied"], 1)
            t.matmul(bank[7][:, 128:144], wT, attn_bd, start=True, stop=True).then_inc(G["wa_ready"], 1)
            pe.wait_ge(G["w_ready"], 1)

            def node_lin(s, weights, width):
                pe.sem_inc(s["turned"], BU)
                with pe.Fori(0, BI) as q:
                    for j in range(BU):
                        pe.wait_ge(s["norm"], q * BU + (j + 1))
                        t.transpose(bank[j // 4][:, (j % 4) * P:(j % 4) * P + P], h_sb[:, j, :], ident[:, :])\
                            .then_inc(s["turned"], 1)
                    pe.wait_ge(s["turned_sb"], q + 1)
                    for j in range(BU):
                        mm = t.matmul(bank[2 + j // 3][:, (j % 3) * 144:(j % 3) * 144 + width], hT_sb[:, j, :], weights,
                                      start=True, stop=True)
                    mm.then_inc(s["lin"], 1)

            node_lin(s_in, w_aug[:, :], 144)

            pe.wait_ge(G["top_turned"], 1)
            t.transpose(bank[6][0:16, 0:P], top16, ident[:, :]).then_inc(G["top_turned"], 1)

            pe.wait_ge(G["flags_ready"], 1)
            general = pe.value_load(flags_i[0:1, 1:2], min_val=0, max_val=1)
            passes = pe.value_load(flags_i[0:1, 0:1], min_val=1, max_val=PASSES)
            with pe.If(general > 0):
                with pe.Fori(0, NG) as g:
                    pe.wait_ge(s_max["rows"], g * (16 * T) + 16 * T)
                    pe.wait_ge(s_max["free"], g + 1)
                    for i in range(T):
                        mm = t.transpose(bank[i // 4][0:HEADS, (i % 4) * P:(i % 4) * P + P],
                                         rows[:, 0, i, HIDDEN:ZW], ident[:, :])
                    mm.then_inc(s_max["turned"], 1)
                with pe.Fori(0, NB) as b:
                    hold(pe, s_max["staged"], b + 1)
                    t.transpose(bank[2][:, 0:HEADS], stage_max, ident[0:HEADS, 0:HEADS]).then_inc(s_max["blk"], 1)

            with pe.Fori(0, passes) as k:
                with pe.Fori(0, GI) as q:
                    n = pe.snap(k * GI + q, min_val=0, max_val=PASSES * GI)

                    def turn(s):
                        pe.wait_ge(s_l1["hot"], n * U + (s + 1))
                        for j in range(HT):
                            mm = t.transpose(bank[0][0:2 * WIN, j * P:(j + 1) * P],
                                             hot[:, s, 2 * j:2 * j + 2, :].rearrange("p t w -> p (t w)"), ident[:, :])
                        mm.then_inc(s_l1["turned"], 1)

                    def targets_er(s):
                        h = s % 2
                        pe.wait_ge(s_l1["hot_turned"], n * U + (s + 1))
                        pe.wait_ge(s_l1["in"][s], n * 32 + 32)
                        for j in range(HT):
                            mm = t.matmul(bank[6 + h][:, j * 32:j * 32 + 32],
                                          hotT[0:2 * WIN, h, j * P:(j + 1) * P],
                                          er_win[0:2 * WIN, s, :], start=True, stop=True)
                        mm.then_inc(s_l1["er"], 1)

                    def sums(s, hf):
                        h = s % 2
                        for i in range(hf * HT, hf * HT + HT):
                            if i % HT == 0:
                                pe.wait_ge(s_l1["msg"], (n * U + s) * 2 + (i // HT + 1))
                            t.matmul(bank[2 + h][:, 0:WIN], msg[:, h, i, :], hot[:, s, i, :],
                                     start=(i == 0), stop=(i == T - 1))
                            mm = t.matmul(bank[4 + h][0:HEADS, 0:WIN], a_sb[:, h, i, :], hot[:, s, i, :],
                                          start=(i == 0), stop=(i == T - 1))
                        if hf == 1:
                            mm.then_inc(s_l1["agg"], 1)

                    turn(0)
                    targets_er(0)
                    for s in range(U):
                        if s + 1 < U:
                            turn(s + 1)
                        sums(s, 0)
                        if s + 1 < U:
                            targets_er(s + 1)
                        sums(s, 1)

            pe.wait_ge(G["up_w_ready"], 1)
            pe.sem_inc(s_mid["agg"], BU)
            with pe.Fori(0, BI) as q:
                pe.wait_ge(s_mid["agg_used"], q + 1)
                for j in range(BU):
                    pe.wait_ge(s_mid["agg_staged"], q * BU + (j + 1))
                    t.transpose(bank[5 + j // 4][:, (j % 4) * P:(j % 4) * P + P], h_sb[:, j, :], ident[:, :])
                    t.transpose(bank[7][:, j * HEADS:(j + 1) * HEADS], hT_sb[0:HEADS, j, :], ident[0:HEADS, 0:HEADS])\
                        .then_inc(s_mid["agg"], 1)
            node_lin(s_mid, w_up[:, :], HIDDEN)

            pe.wait_ge(loads["mlp"], 160)
            pe.sem_inc(s_l2["half_free"], 2)

            def hidden1(s, arrived):
                pe.wait_ge(s_l2["in"][s], arrived)
                t.matmul(bank[4], a1_bd[:, :], ef_sb[:, s, :], start=True, stop=True).then_inc(s_l2["h1"], 1)

            def hidden2(m):
                pe.wait_ge(s_l2["h1_act"], m + 1)
                t.matmul(bank[5], a2_bd[:, :], h1_sb, start=True, stop=True).then_inc(s_l2["h2"], 1)

            def radial(m, h):
                pe.wait_ge(s_l2["h2_act"], m + 1)
                for j in range(HT):
                    mm = t.matmul(bank[2 * h + j // 2][:, (j % 2) * 256:(j % 2) * 256 + 256],
                                  h2_sb[:, h, j * P:(j + 1) * P], a3_bd[:, :], start=True, stop=True)
                mm.then_inc(s_l2["tp"], 1)

            with pe.Fori(0, passes) as k:
                hidden1(0, k * (32 * (GI + 1)) + 32)
                hidden2(k * (NG + 1))
                radial(k * (NG + 1), 0)
                with pe.Fori(0, GI) as q:
                    n = pe.snap(k * GI + q, min_val=0, max_val=PASSES * GI)
                    m = pe.snap(k * (NG + 1) + q * U, min_val=0, max_val=PASSES * (NG + 1))

                    def sums(s, hf):
                        h = s % 2
                        pe.wait_ge(s_l2["prod"], n * (2 * U) + (2 * s + hf + 1))
                        for j in range(HT):
                            st, en = (hf + j == 0), (hf == 1 and j == HT - 1)
                            t.matmul(bank[6 + h][:, 0:WIN], prod[:, hf, j, 0, :], wy[:, hf, j, 0:WIN],
                                     start=st, stop=en, skip_group_check=True)
                            mm = t.matmul(bank[6 + h][:, WIN:4 * WIN], prod[:, hf, j, 1, :],
                                          wy[:, hf, j, WIN:4 * WIN], start=False, stop=en, skip_group_check=True)
                        mm.then_inc(s_l2["half_free"], 1)

                    for s in range(U):
                        if s + 1 < U:
                            hidden1(s + 1, n * 32 + 32)
                        else:
                            hidden1(0, (n + k) * 32 + 64)
                        sums(s, 0)
                        hidden2(m + (s + 1))
                        sums(s, 1)
                        radial(m + (s + 1), (s + 1) % 2)

            pe.wait_ge(G["out_w_ready"], 3)
            pe.sem_inc(s_out["agg"], BU)
            pe.sem_inc(s_out["added"], BU)
            with pe.Fori(0, BI) as q:
                for j in range(BU):
                    pe.wait_ge(s_out["agg_staged"], q * BU + (j + 1))
                    pe.wait_ge(s_out["turned_sb"], q * BU + (j + 1))
                    pe.wait_ge(s_out["added"], q * BU + (j + 1))
                    for c in range(4):
                        mm = t.matmul(bank[j][:, 0:P], stage[:, j, c, :], wo_a[:, :] if c == 0 else wo_b[:, c - 1, :],
                                      start=(c == 0), stop=(c == 3))
                    mm.then_inc(s_out["agg"], 1)


def kernel(x, src, dst, edge_attr_4, edge_attr_8, **w):
    import numpy as np
    import concourse.bacc as bacc
    from concourse.bass_utils import run_bass_kernel_spmd

    extra = NG * GE - EDGES
    more = extra + GE
    arrays = {
        "x": np.concatenate([np.asarray(x), np.zeros((NB * P - NODES, HIDDEN), np.float32)]),
        "src": np.concatenate([np.asarray(src), np.zeros(extra, np.int32)]).reshape(NG, P, T),
        "dst": np.concatenate([np.asarray(dst), np.full(extra, PAD_DST, np.int32)]).reshape(NG, P, T),
        "edge_y": np.concatenate([np.asarray(edge_attr_4), np.zeros((more, 4), np.float32)])
            .reshape(NG + 1, P, T * 4),
        "edge_f": np.ascontiguousarray(
            np.concatenate([np.asarray(edge_attr_8), np.zeros((more, 8), np.float32)])
            .reshape(NG + 1, P, 2, HT, 8).transpose(0, 2, 4, 3, 1)).reshape(NG + 1, 16, HT * P),
    }
    for name, key in (("W", "L0_gnn_W"), ("attn_l", "L0_gnn_attn_l"), ("attn_r", "L0_gnn_attn_r"),
                      ("bias", "L0_gnn_bias"), ("W_up_s", "L1_gnn_W_up_s"), ("W_up_v", "L1_gnn_W_up_v"),
                      ("A1", "L1_gnn_A1"), ("b1", "L1_gnn_b1"), ("A2", "L1_gnn_A2"), ("b2", "L1_gnn_b2"),
                      ("A3", "L1_gnn_A3"), ("W_out_s", "L1_gnn_W_out_s"), ("W_out_v", "L1_gnn_W_out_v")):
        arrays[name] = np.ascontiguousarray(w[key])
    arrays["identity"] = np.concatenate([np.eye(P, dtype=np.float32),
                                         np.tile(np.arange(WIN + 2, dtype=np.float32), (P, 1))], axis=1)

    nc = bacc.Bacc("TRN2", target_bir_lowering=False, num_devices=1)
    args = [nc.dram_tensor(f"in_{n}", a.shape, mybir.dt.from_np(a.dtype), kind="ExternalInput").ap()
            for n, a in arrays.items()]
    out = nc.dram_tensor("out", (NODES, HIDDEN), F32, kind="ExternalOutput").ap()
    gnn_kernel(nc, *args, out)
    r = run_bass_kernel_spmd(nc, [{f"in_{n}": a for n, a in arrays.items()}], core_ids=[0])
    return r.results[0]["out"]
```

```python
from contextlib import ExitStack

import concourse.bass as bass
from concourse import mybir

F32 = mybir.dt.float32
I32 = mybir.dt.int32
ALU = mybir.AluOpType
ACT = mybir.ActivationFunctionType
AX = mybir.AxisListType

P = 128
NODES, EDGES, HIDDEN, HEADS, MUL = 6250, 200000, 128, 8, 32
PER_HEAD = HIDDEN // HEADS
NEG_SLOPE = 0.2
EPS = 1e-5

NB = -(-NODES // P)
BU = 7
BI = NB // BU
HALVES = ((0, 4), (4, BU))
SLOTS = 4
REUSED = BI - SLOTS
TAIL = NODES - (NB - 1) * P
COLS = (NB + 1) * P
PAD_DST = COLS - 1

T = 8
HT = T // 2
GE = T * P
NG = EDGES // GE + 1
U = 4
AHEAD = 2
GI = NG // U
NG2 = NG // 2
WIN = 48
PASSES = -(-NODES // WIN)
SPREAD = 80.0
TINY = 1e-36
ZW = HIDDEN + HEADS

assert NB - 1 <= WIN
assert NB == BU * BI and NG == U * GI and NG * GE >= EDGES and PAD_DST >= NODES + WIN


def bc(ap, axis, n):
    wide = ap.unsqueeze(axis)
    shape = list(wide.shape)
    shape[axis] = n
    return wide.broadcast_to(shape)


def gnn_kernel(nc, x, src, dst, edge_y, edge_f, W, attn_l, attn_r, bias, W_up_s, W_up_v, A1, b1, A2, b2, A3,
               W_out_s, W_out_v, identity, out):
    with ExitStack() as ctx:
        def sb(name, shape, dt=F32):
            return ctx.enter_context(nc.sbuf_tensor(name, shape, dt))

        def sem(name):
            return ctx.enter_context(nc.semaphore(name))

        def sems(name, n):
            return [sem(f"{name}{i}") for i in range(n)]

        def dram(name, shape, dt=F32):
            return nc.dram_tensor(name, shape, dt, kind="Internal").ap()

        z_tab = dram("z_tab", (NB * P, ZW))
        er_tab = dram("er_tab", (COLS, 2 * HEADS))
        up_tab = dram("up_tab", (NB * P, HIDDEN))
        win_dram = dram("win_dram", (2 * NG,))

        pair = [ctx.enter_context(nc.psum_tensor(f"pair{i}", [P, 2, 512], F32)) for i in range(4)]
        bank = [pair[i // 2][:, i % 2, :] for i in range(8)]

        x_sb = sb("x_sb", [P, NB, HIDDEN])
        acc_a = sb("acc_a", [P, COLS])
        acc_b = sb("acc_b", [P, 3, COLS])
        den_acc = acc_b[0:HEADS, 0, :]
        max_acc = acc_b[0:HEADS, 1, :]
        dst_rel = sb("dst_rel", [P, NG + 1, T])
        win_f = sb("win_f", [P, NG])
        win_i = sb("win_i", [1, 1 + NG + AHEAD], I32)
        ready = sb("ready", [1, GI + 2], I32)
        ident = sb("ident", [P, P])
        iota = sb("iota", [P, WIN])
        ones = sb("ones", [2 * HEADS, P])
        flags = sb("flags", [P, 8])
        flags_i = sb("flags_i", [1, 2], I32)
        vec = sb("vec", [P, 8])
        bias_bc = sb("bias_bc", [P, HIDDEN])
        w_aug = sb("w_aug", [P, 144])
        w_up = sb("w_up", [P, HIDDEN])
        a1_bd = sb("a1_bd", [16, P])
        a2_bd = sb("a2_bd", [P, P])
        a3_bd = sb("a3_bd", [P, 2 * P])
        wo_a = sb("wo_a", [P, HIDDEN])
        wo_b = sb("wo_b", [P, 3, HIDDEN])
        rows = sb("rows", [P, U, T, ZW])
        idx = sb("idx", [P, U, T], I32)
        idx_max = sb("idx_max", [P, T], I32)
        er_win = sb("er_win", [P, U, 4 * HEADS])
        y_sb = sb("y_sb", [P, U, T, 4])
        ef_sb = sb("ef_sb", [16, U, HT * P])

        share = sb("share", [P, 7424])

        def part(at, *shape, parts=P):
            n = 1
            for s in shape:
                n *= s
            flat = share[0:parts, at:at + n]
            names = "abcd"[:len(shape)]
            if len(shape) == 1:
                return flat
            return flat.rearrange(f"p ({' '.join(names)}) -> p {' '.join(names)}",
                                  **{c: s for c, s in zip(names[1:], shape[1:])})

        h_sb = part(0, BU, P)
        hT_sb = part(896, BU, P)
        tab_sb = rows[:, :, :, :].rearrange("p u t f -> p (u t) f")
        stats = part(2800, BU, 6)
        mv = part(2842, BU, 2)
        mv_all = part(7168, NB, 2)
        std = part(7266, NB)
        rstd = part(7315, NB)
        nmr = part(7364, NB)
        elr = part(3000, NB, 2 * HEADS)
        erm = part(3784, NB, 2 * HEADS)
        top = part(4568, NB, HEADS)
        dst_i = part(4960, NG, T).bitcast(I32)
        redn = part(6528, 2, NG)
        wide = part(6528, 2 * NG)
        cols4 = part(6920, 4, parts=NG2)
        top16 = part(6924, 2 * HEADS)
        top_bc = part(6940, 2 * HEADS)
        wT = part(6960, P)
        attn_bd = part(7088, 2 * HEADS)
        stage_max = part(2048, P, parts=HEADS)
        elT_sb = part(0, GE, parts=HEADS)
        dst_row = part(1024, GE, parts=1).bitcast(I32)
        hot = part(0, U, T, WIN)
        hotT = part(1536, 2, 512)
        msg = part(2560, 2, T, P)
        e_sb = part(4608, 4, T * HEADS)
        a_sb = part(4864, 2, T, HEADS)
        num_stage = part(4992, P)
        den_stage = part(5120, P, parts=HEADS)
        part_row = part(5248, P)
        rden = part(5376, HEADS)
        stats1 = part(5384, 6)
        mv1 = part(5390, 2)
        eq = part(0, 2, HT, WIN)
        wy = part(512, 2, HT, 4 * WIN)
        prod = part(2560, 2, HT, 2, P)
        h1_sb = part(4608, 512)
        h2_sb = part(5120, 2, 512)
        stage = part(2048, 4, P)
        least = part(0, GI, parts=1)
        ends = part(64, NB - 1, parts=1)
        past = part(128, GI, NB - 1, parts=1)

        loads = {n: sem(f"load_{n}") for n in
                 ("x0", "x1", "const", "dst", "w", "attn", "bias", "mlp", "up", "out_w", "win")}
        zeroed = sem("zeroed")
        G = {n: sem(n) for n in (
            "red_ready", "red_turned", "cols_ready", "win_stored", "wT_ready", "wT_copied", "attn_ready", "wa_ready",
            "w_ready", "top_ready", "top_turned", "top_bc_ready", "flags_ready", "er_stored", "er_ready_tab",
            "pass_set", "ready_set", "out_w_ready", "up_w_ready")}

        def named(tag, names):
            return {n: sem(f"{tag}_{n}") for n in names}

        node_steps = ("var", "std", "stat", "norm", "turned", "turned_sb", "lin", "row", "stored", "stored_early")
        s_in = named("in", node_steps)
        s_mid = named("mid", node_steps + ("agg_staged", "agg", "agg_used"))
        s_out = named("out", ("agg_staged", "agg", "added", "stored"))

        def edge_sems(tag, names):
            return named(tag, ("rows_free", "added", "open", "landed") + names) \
                | {n: sems(f"{tag}_{n}_slot", U) for n in ("rows", "in")}

        s_idx = sems("idx", U)
        s_l1 = edge_sems("l1", ("hot", "turned", "hot_turned", "er", "score", "exp", "msg", "agg"))
        s_l2 = edge_sems("l2", ("h1", "h1_act", "h2", "h2_act", "tp", "prod", "half_free"))
        s_max = named("max", ("idx", "rows", "dst", "free", "turned", "taken", "col", "staged", "blk", "top"))

        block = ctx.enter_context(nc.Block())
        passed = sem("passed")

        def plain_wait(eng, s, value):
            eng.wait_ge(s, value)

        def hold(eng, s, value):
            eng.wait_ge(s, value)
            eng.sem_inc(passed, 1)

        def blocks(eng, at, work):
            lo = eng.value_load(ready[0:1, bass.ds(at, 1)], min_val=0, max_val=NB - 1)
            hi = eng.value_load(ready[0:1, bass.ds(at + 1, 1)], min_val=0, max_val=NB - 1)
            with eng.If(hi > lo):
                with eng.Fori(lo, hi) as b:
                    work(b)
            return hi

        def last_blocks(eng, work):
            lo = eng.value_load(ready[0:1, GI + 1:GI + 2], min_val=0, max_val=NB - 1)
            with eng.Fori(lo, NB) as b:
                work(b)

        class Own:

            def __init__(self, eng, s):
                self.eng, self.s, self.n, self.base = eng, s, 0, None

            def mark(self, ins):
                ins.then_inc(self.s, 1)
                self.n += 1
                return self.n if self.base is None else self.base + self.n

            def after(self, ins, wait=plain_wait):
                wait(self.eng, self.s, self.mark(ins))

        @block.sync
        def _(sp):
            for c in range(BI):
                sp.dma_start(x_sb[:, c * BU:(c + 1) * BU, :],
                             x[c * BU * P:(c + 1) * BU * P, :].rearrange("(k p) f -> p k f", p=P))\
                  .then_inc(loads["x0" if c < BI // 2 else "x1"], 16)
            sp.dma_start(ident[:, :], identity[:, 0:P]).then_inc(loads["const"], 16)
            sp.dma_start(iota[:, :], identity[:, P:P + WIN]).then_inc(loads["const"], 16)
            sp.dma_start(w_aug[:, 0:HIDDEN], W).then_inc(loads["w"], 16)
            for n, a in enumerate((attn_l, attn_r)):
                sp.dma_start(vec[:, n:n + 1], a.rearrange("h (p a) -> (h p) a", a=1)).then_inc(loads["attn"], 16)
            sp.dma_start(bias_bc[:, :], bias.partition_broadcast(P)).then_inc(loads["bias"], 16)
            sp.wait_ge(zeroed, 7)
            for half in range(2):
                sp.dma_start(a1_bd[8 * half:8 * half + 8, 64 * half:64 * half + 64], A1).then_inc(loads["mlp"], 16)
                sp.dma_start(a2_bd[64 * half:64 * half + 64, 64 * half:64 * half + 64], A2).then_inc(loads["mlp"], 16)
                sp.dma_start(a3_bd[64 * half:64 * half + 64, P * half:P * half + P], A3).then_inc(loads["mlp"], 16)
                for n, b in enumerate((b1, b2)):
                    sp.dma_start(vec[64 * half:64 * half + 64, 2 + n:3 + n], b.rearrange("(n a) -> n a", a=1))\
                      .then_inc(loads["mlp"], 16)
            sp.dma_start(w_up[0:MUL, 96:128], W_up_s).then_inc(loads["up"], 16)
            sp.dma_start(wo_a[96:128, 0:MUL], W_out_s[0:MUL, :]).then_inc(loads["out_w"], 16)
            for i in range(3):
                sp.dma_start(w_up[MUL + i:P:3, MUL * i:MUL * i + MUL], W_up_v).then_inc(loads["up"], 16)
                vcols = wo_a[MUL * i:MUL * i + MUL, MUL + i:P:3]
                sp.dma_start(vcols, W_out_v[MUL:2 * MUL, :], allow_slow_non_contiguous=True).then_inc(loads["out_w"], 16)
                sp.dma_start(wo_b[MUL * i:MUL * i + MUL, i, 0:MUL], W_out_s[MUL:2 * MUL, :])\
                  .then_inc(loads["out_w"], 16)
                sp.dma_start(wo_b[96:128, i, MUL + i:P:3], W_out_v[0:MUL, :],
                             allow_slow_non_contiguous=True).then_inc(loads["out_w"], 16)

            sp.wait_ge(G["cols_ready"], 1)
            for n, c in enumerate(cols4[0:NG2, i:i + 1] for i in range(4)):
                sp.dma_start(win_dram[NG2 * n:NG2 * n + NG2].rearrange("(n a) -> n a", a=1), c)\
                  .then_inc(G["win_stored"], 16)
            sp.wait_ge(G["win_stored"], 64)
            sp.dma_start(wide, win_dram.partition_broadcast(P)).then_inc(loads["win"], 16)

            def store_rows(s, width, tab):
                for first, last, moved, stored in ((0, REUSED, 0, "stored_early"), (REUSED, SLOTS, 0, "stored"),
                                                   (SLOTS, BI, SLOTS, "stored")):
                    with sp.Fori(first, last) as q:
                        sp.wait_ge(s["row"], q + 1)
                        sp.dma_start(tab[bass.ds(q * (BU * P), BU * P), :].rearrange("(k p) f -> p k f", p=P),
                                     tab_sb[:, bass.ds((q - moved) * BU, BU), 0:width]).then_inc(s[stored], 16)

            for s in range(U):
                sp.dma_start(idx[:, s, :], src[s, :, :]).then_inc(s_idx[s], 16)
            store_rows(s_in, ZW, z_tab)

            def load_idx(s, group):
                sp.dma_start(idx[:, s, :], src[bass.ds(group, 1), :, :].rearrange("a p t -> (a p) t"))\
                  .then_inc(s_idx[s], 16)

            sp.wait_ge(G["flags_ready"], 1)
            general = sp.value_load(flags_i[0:1, 1:2], min_val=0, max_val=1)
            with sp.If(general > 0):
                with sp.Fori(0, NG) as g:
                    sp.wait_ge(s_max["free"], g + 1)
                    sp.dma_start(idx_max[:, :], src[bass.ds(g, 1), :, :].rearrange("a p t -> (a p) t"))\
                      .then_inc(s_max["idx"], 16)
                    sp.dma_start(dst_row.rearrange("a (t p) -> a t p", t=T),
                                 dst[:, bass.ds(g, 1), :].rearrange("p a t -> a t p"),
                                 allow_slow_non_contiguous=True).then_inc(s_max["dst"], 16)

            sp.wait_ge(G["er_ready_tab"], 1)
            sp.dma_start(er_tab[0:NB * P, :].rearrange("(k p) f -> p k f", p=P), erm).then_inc(G["er_stored"], 16)
            sp.dma_start(er_tab[NB * P:COLS, :], acc_b[:, 2, 0:2 * HEADS]).then_inc(G["er_stored"], 16)
            sp.wait_ge(G["er_stored"], 32)

            passes = sp.value_load(flags_i[0:1, 0:1], min_val=1, max_val=PASSES)

            def load_window(s, group):
                w0 = sp.value_load(win_i[0:1, bass.ds(group + 1, 1)], min_val=0, max_val=COLS - WIN)
                for half in range(2):
                    sp.dma_start(er_win[WIN * half:WIN * half + WIN, s, 16 * half:16 * half + 16],
                                 er_tab[bass.ds(w0, WIN), :]).then_inc(s_l1["in"][s], 16)

            def edge_loads(s_l, load, q, n):
                for s in range(U):
                    i = n * U + s
                    hold(sp, s_l["rows_free"], i + (1 + AHEAD))
                    load((s + AHEAD) % U, q * U + (s + AHEAD))
                    hold(sp, s_l["landed"], i + 1)
                    load_idx(s, q * U + (s + U))

            with sp.Fori(0, passes) as k:
                hold(sp, G["pass_set"], k + 1)
                for s in range(AHEAD):
                    load_window(s, s)
                with sp.Fori(0, GI) as q:
                    n = sp.snap(k * GI + q, min_val=0, max_val=PASSES * GI)
                    edge_loads(s_l1, load_window, q, n)
                for s in range(AHEAD):
                    hold(sp, s_l1["in"][s], (k + 1) * (32 * (GI + 1)))
                hold(sp, s_l1["er"], (k + 1) * (NG + 1))

            store_rows(s_mid, HIDDEN, up_tab)

            def store_block(b):
                sp.wait_ge(s_out["added"], b + 1)
                sp.dma_start(out[bass.ds(b * P, P), :],
                             x_sb[:, bass.ds(b, 1), :].rearrange("p a f -> p (a f)")).then_inc(s_out["stored"], 16)

            def load_edges(s, group):
                sp.dma_start(y_sb[:, s, :, :].rearrange("p t k -> p (t k)"),
                             edge_y[bass.ds(group, 1), :, :].rearrange("a p t -> (a p) t")).then_inc(s_l2["in"][s], 16)
                sp.dma_start(ef_sb[:, s, :], edge_f[bass.ds(group, 1), :, :].rearrange("a p t -> (a p) t"))\
                  .then_inc(s_l2["in"][s], 16)

            sp.wait_ge(G["ready_set"], 1)
            with sp.Fori(0, passes) as k:
                for s in range(AHEAD):
                    load_edges(s, s)
                with sp.Fori(0, GI) as q:
                    n = sp.snap(k * GI + q, min_val=0, max_val=PASSES * GI)
                    edge_loads(s_l2, load_edges, q, n)
                    blocks(sp, q, store_block)
                hold(sp, s_l2["h1"], (k + 1) * (NG + AHEAD))

            stored = sp.value_load(ready[0:1, GI:GI + 1], min_val=0, max_val=NB - 1)
            with sp.If(stored < NB - 1):
                with sp.Fori(stored, NB - 1) as b:
                    store_block(b)
            sp.wait_ge(s_out["added"], NB)
            sp.dma_start(out[(NB - 1) * P:NODES, :], x_sb[0:TAIL, NB - 1, :]).then_inc(s_out["stored"], 16)
            sp.wait_ge(s_out["stored"], 16 * NB)

        @block.gpsimd
        def _(pool):
            for z in (a1_bd, a2_bd, a3_bd, wo_a, wo_b, w_up):
                pool.memset(z[:], 0.0).then_inc(zeroed, 1)
            pool.memset(er_win[:], 0.0).then_inc(zeroed, 1)
            pool.memset(acc_b[:], 0.0).then_inc(zeroed, 1)
            pool.memset(acc_a[:], 0.0).then_inc(zeroed, 1)
            pool.memset(win_i[:], 0).then_inc(zeroed, 1)

            def gather(s, indices, table, width, done):
                for t in range(T):
                    pool.indirect_dma_start(out=rows[:, s, t, 0:width], out_offset=None, in_=table,
                                            in_offset=bass.IndirectOffsetOnAxis(ap=indices[:, t:t + 1], axis=0))\
                        .then_inc(done, 16)

            pool.wait_ge(G["flags_ready"], 1)
            general = pool.value_load(flags_i[0:1, 1:2], min_val=0, max_val=1)
            passes = pool.value_load(flags_i[0:1, 0:1], min_val=1, max_val=PASSES)
            def table_stored(s):
                pool.wait_ge(s["stored_early"], 16 * REUSED)
                pool.wait_ge(s["stored"], 16 * (BI - REUSED))

            table_stored(s_in)
            with pool.If(general > 0):
                with pool.Fori(0, NG) as g:
                    hold(pool, s_max["idx"], (g + 1) * 16)
                    gather(0, idx_max, z_tab, ZW, s_max["rows"])
                hold(pool, s_max["free"], NG + 1)

            for s_l, tab, width in ((s_l1, z_tab, ZW), (s_l2, up_tab, HIDDEN)):
                if s_l is s_l2:
                    pool.wait_ge(s_mid["agg_staged"], NB)
                    pool.memset(den_acc, 0.0).then_inc(zeroed, 1)
                    pool.memset(max_acc, 0.0).then_inc(zeroed, 1)
                    pool.memset(acc_a[:], 0.0).then_inc(zeroed, 1)
                    table_stored(s_mid)
                before = 0 if s_l is s_l1 else passes * GI
                with pool.Fori(0, passes) as k:
                    pool.sem_inc(s_l["open"], 1)
                    with pool.Fori(0, GI) as q:
                        n = pool.snap(k * GI + q, min_val=0, max_val=PASSES * GI)
                        for s in range(U):
                            hold(pool, s_idx[s], (n + before) * 16 + 16)
                            hold(pool, s_l["rows_free"], n * U + (s + 1))
                            gather(s, idx[:, s, :], tab, width, s_l["rows"][s])
                    for s in range(U):
                        hold(pool, s_l["rows"][s], GI * 16 * T)
                    hold(pool, s_l["rows_free"], (k + 1) * NG + U)
                    pool.inc_swdge_sem(s_l["rows"], [GI * 16 * T] * U, mode="sub")

        @block.scalar
        def _(act):
            def node_norm(s):
                act.wait_ge(s["var"], 1)
                nc.scalar.activation(std, mv_all[:, :, 1], ACT.Sqrt, bias=flags[:, 7:8]).then_inc(s["std"], 1)
                act.wait_ge(s["stat"], 1)
                with act.Fori(0, BI) as q:
                    for j in range(BU):
                        act.wait_ge(s["turned"], q * BU + (j + 1))
                        at = bass.ds(q * BU + j, 1)
                        nc.scalar.activation(h_sb[:, j, :], x_sb[:, at, :].rearrange("p a f -> p (a f)"), ACT.Relu,
                                             bias=nmr[:, at], scale=rstd[:, at]).then_inc(s["norm"], 1)

            act.dma_start(dst_i, dst).then_inc(loads["dst"], 16)
            act.wait_ge(G["wT_ready"], 1)
            nc.scalar.activation(wT, bank[7][:, 0:P], ACT.Copy).then_inc(G["wT_copied"], 1)
            act.wait_ge(G["wa_ready"], 1)
            nc.scalar.activation(w_aug[:, HIDDEN:144], bank[7][:, 128:144], ACT.Copy).then_inc(G["w_ready"], 1)
            node_norm(s_in)

            act.wait_ge(G["flags_ready"], 1)
            passes = act.value_load(flags_i[0:1, 0:1], min_val=1, max_val=PASSES)

            def stage_sums(b):
                act.wait_ge(s_mid["agg"], b + 1)
                nc.scalar.activation(num_stage, acc_a[:, bass.ds(b * P, P)], ACT.Copy)
                nc.scalar.activation(den_stage, den_acc[:, bass.ds(b * P, P)], ACT.Copy)\
                    .then_inc(s_mid["agg_staged"], 1)

            act.wait_ge(G["ready_set"], 1)
            def copy_turned(s, m):
                act.wait_ge(s_l1["turned"], m + 1)
                nc.scalar.activation(hotT[0:2 * WIN, s % 2, :], bank[0][0:2 * WIN, :], ACT.Copy)\
                    .then_inc(s_l1["hot_turned"], 1)

            with act.Fori(0, passes) as k:
                copy_turned(0, k * (NG + 1))
                with act.Fori(0, GI) as q:
                    n = act.snap(k * GI + q, min_val=0, max_val=PASSES * GI)
                    m = act.snap(k * (NG + 1) + q * U, min_val=0, max_val=PASSES * (NG + 1))
                    for s in range(U):
                        h = s % 2
                        act.wait_ge(s_l1["score"], n * U + (s + 1))
                        nc.scalar.activation(a_sb[:, h, :, :].rearrange("p t h -> p (t h)"), e_sb[:, 3, :], ACT.Exp)\
                            .then_inc(s_l1["exp"], 1)
                        copy_turned(s + 1, m + (s + 1))
                        if s == 1:
                            hold(act, s_l1["added"], n * U + 1)
                            blocks(act, q + 1, stage_sums)

            hold(act, s_l1["added"], passes * NG + 1)
            last_blocks(act, stage_sums)
            node_norm(s_mid)

            def hidden(m, h):
                act.wait_ge(s_l2["h1"], m + 1)
                nc.scalar.activation(h1_sb, bank[4], ACT.Silu, bias=vec[:, 2:3]).then_inc(s_l2["h1_act"], 1)
                act.wait_ge(s_l2["h2"], m + 1)
                nc.scalar.activation(h2_sb[:, h, :], bank[5], ACT.Silu, bias=vec[:, 3:4]).then_inc(s_l2["h2_act"], 1)

            def stage_block(b):
                act.wait_ge(s_out["agg"], b + 1)
                nc.scalar.activation(stage[:, 0, :], acc_a[:, bass.ds(b * P, P)], ACT.Copy)
                nc.scalar.activation(stage[:, 1:4, :], acc_b[:, :, bass.ds(b * P, P)], ACT.Copy)\
                    .then_inc(s_out["agg_staged"], 1)

            with act.Fori(0, passes) as k:
                for s in range(AHEAD):
                    hidden(k * (NG + AHEAD) + s, s)
                with act.Fori(0, GI) as q:
                    n = act.snap(k * GI + q, min_val=0, max_val=PASSES * GI)
                    m = act.snap(k * (NG + AHEAD) + q * U, min_val=0, max_val=PASSES * (NG + AHEAD))
                    for s in range(U):
                        hidden(m + (s + AHEAD), s % 2)
                        if s == 0:
                            hold(act, s_l2["added"], n * U + 1)
                            blocks(act, q + 1, stage_block)

            hold(act, s_l2["added"], passes * NG + 1)
            last_blocks(act, stage_block)

        @block.vector
        def _(dve):
            own = Own(dve, sem("own_set_up"))
            v = nc.vector

            v.memset(flags[:, 7:8], EPS)
            v.memset(dst_rel[:, NG, :], 0.0)
            v.memset(ones[:, :], 1.0).then_inc(G["top_ready"], 1)
            dve.sem_inc(s_l1["rows_free"], U)
            dve.sem_inc(s_l2["rows_free"], U)

            def norm_stats(q):
                done = []
                for lo, hi in HALVES:
                    for j in range(lo, hi):
                        ins = v.bn_stats(stats[:, j, :],
                                         x_sb[:, bass.ds(q * BU + j, 1), :].rearrange("p a f -> p (a f)"))
                    done.append(own_loop.mark(ins))
                for (lo, hi), stats_mark in zip(HALVES, done):
                    hold(dve, own_loop.s, stats_mark)
                    for j in range(lo, hi):
                        ins = v.bn_aggr(mv[:, j, :], stats[:, j, :])
                own_loop.after(ins)
                own_loop.mark(v.tensor_copy(mv_all[:, bass.ds(q * BU, BU), :], mv))

            def stats_of_x(first, last, loaded):
                dve.wait_ge(loaded, 16 * (last - first))
                with dve.Fori(first, last) as q:
                    own_loop.base, own_loop.n = q * 4, 0
                    norm_stats(q)
                    assert own_loop.n == 4

            dve.wait_ge(loads["dst"], 16)
            own.after(v.tensor_copy(dst_rel[:, 0:NG, :], dst_i))
            own.after(v.tensor_reduce(redn[:, 0, :], dst_rel[:, 0:NG, :], AX.X, ALU.min))
            own.after(v.scalar_tensor_tensor(out=dst_i.bitcast(F32), in0=dst_rel[:, 0:NG, :], scalar=float(NODES),
                                             in1=dst_rel[:, 0:NG, :], op0=ALU.is_lt, op1=ALU.mult))
            v.tensor_reduce(redn[:, 1, :], dst_i.bitcast(F32), AX.X, ALU.max).then_inc(G["red_ready"], 1)

            own_loop = Own(dve, sem("own_in"))
            stats_of_x(0, BI // 2, loads["x0"])

            dve.wait_ge(loads["attn"], 32)
            dve.wait_ge(loads["const"], 32)
            head = top_bc
            v.tensor_reduce(head[:, 0:HEADS], ident[:, :].rearrange("p (h q) -> p h q", q=PER_HEAD), AX.X, ALU.max)\
                .then_inc(G["attn_ready"], 1)
            dve.wait_ge(G["attn_ready"], 1)
            for n in range(2):
                v.tensor_scalar(attn_bd[:, 8 * n:8 * n + 8], head[:, 0:HEADS], vec[:, n:n + 1], None, ALU.mult)\
                    .then_inc(G["attn_ready"], 1)
            dve.wait_ge(G["red_turned"], 1)
            own.after(v.tensor_reduce(cols4[:, 0:2], bank[5][0:NG2, 0:256].rearrange("p (a b) -> p a b", b=P), AX.X,
                                      ALU.min))
            own.after(v.tensor_reduce(cols4[:, 2:4], bank[5][0:NG2, 256:512].rearrange("p (a b) -> p a b", b=P), AX.X,
                                      ALU.max))
            v.tensor_tensor(cols4[:, 2:4], cols4[:, 2:4], cols4[:, 0:2], ALU.subtract).then_inc(G["cols_ready"], 1)

            def scale_weights():
                inv, inv2 = MUL ** -0.5, (2 * MUL) ** -0.5
                dve.wait_ge(loads["up"], 64)
                v.tensor_scalar(w_up[:, :], w_up[:, :], inv, None, ALU.mult).then_inc(G["up_w_ready"], 1)
                dve.wait_ge(loads["out_w"], 160)
                v.tensor_scalar(wo_a[:, :], wo_a[:, :], inv2 / 10.0, None, ALU.mult).then_inc(G["out_w_ready"], 1)
                v.tensor_scalar(wo_b[0:96, :, :], wo_b[0:96, :, :], inv2 / 10.0 / 3.0 ** 0.5, None, ALU.mult)\
                    .then_inc(G["out_w_ready"], 1)
                v.tensor_scalar(wo_b[96:128, :, :], wo_b[96:128, :, :], inv2 / 10.0, None, ALU.mult)\
                    .then_inc(G["out_w_ready"], 1)

            def norm_scale(s, meanwhile=None):
                dve.sem_inc(s["var"], 1)
                if meanwhile is not None:
                    meanwhile()
                dve.wait_ge(s["std"], 1)
                own.after(v.reciprocal(rstd, std))
                v.scalar_tensor_tensor(out=nmr, in0=mv_all[:, :, 0], scalar=-1.0, in1=rstd, op0=ALU.mult,
                                       op1=ALU.mult).then_inc(s["stat"], 1)

            def node_rows(s, width):
                for first, last in ((0, SLOTS), (SLOTS, BI)):
                    if first > 0:
                        dve.wait_ge(s["stored_early"], 16 * REUSED)
                    with dve.Fori(first, last) as q:
                        for b, (lo, hi) in enumerate(HALVES):
                            dve.wait_ge(s["turned"], (q + 1) * BU + hi)
                            v.tensor_copy(hT_sb[:, lo:hi, :].rearrange("p a b -> p (a b)"),
                                          bank[b][:, 0:(hi - lo) * P]).then_inc(s["turned_sb"], 1)
                        for b in range(3):
                            m = min(3, BU - 3 * b)
                            dve.wait_ge(s["lin"], q * BU + (3 * b + m))
                            lin = bank[2 + b][:, 0:m * 144].rearrange("p (a b) -> p a b", b=144)
                            if s is s_in:
                                v.tensor_copy(elr[:, bass.ds(q * BU + 3 * b, m), :], lin[:, :, HIDDEN:144])
                            ins = v.tensor_copy(tab_sb[:, bass.ds((q - first) * BU + 3 * b, m), 0:width],
                                                lin[:, :, 0:width])
                        ins.then_inc(s["row"], 1)

            def set_windows():
                own.after(v.tensor_copy(win_f[:, :], wide[:, 0:NG]))
                own.after(v.tensor_copy(win_i[0:1, 1:NG + 1], win_f[0:1, :]))
                own.after(v.tensor_tensor(dst_rel[:, 0:NG, :], dst_rel[:, 0:NG, :], bc(win_f[:, :], 2, T),
                                          ALU.subtract))

            stats_of_x(BI // 2, BI, loads["x1"])
            dve.wait_ge(own_loop.s, BI * 4)
            norm_scale(s_in, meanwhile=scale_weights)

            dve.wait_ge(loads["win"], 16)
            own.after(v.tensor_reduce(flags[:, 2:3], wide[:, NG:2 * NG], AX.X, ALU.max))
            own.after(v.tensor_scalar(flags[:, 0:1], flags[:, 2:3], WIN - 0.5, None, ALU.is_gt))
            own.after(v.tensor_scalar(flags[:, 5:6], flags[:, 0:1], float(PASSES - 1), 1.0, ALU.mult, ALU.add))
            own.after(v.tensor_copy(flags_i[0:1, 0:1], flags[0:1, 5:6]))
            own.after(v.tensor_scalar(flags[:, 6:7], flags[:, 0:1], -1.0, 1.0, ALU.mult, ALU.add))
            own.after(v.tensor_scalar(wide[:, 0:NG], wide[:, 0:NG], flags[:, 6:7], None, ALU.mult))
            dve.wait_ge(zeroed, 10)
            set_windows()

            node_rows(s_in, ZW)

            dve.wait_ge(s_in["row"], BI)
            ev = elr.rearrange("p k f -> p f k")
            own.after(v.tensor_reduce(top16[:, 0:8], ev[:, 0:8, :], AX.X, ALU.max))
            own.after(v.tensor_reduce(top16[:, 8:16], ev[:, 0:8, :], AX.X, ALU.min))
            v.tensor_scalar(top16[:, 8:16], top16[:, 8:16], -1.0, None, ALU.mult).then_inc(G["top_turned"], 1)
            dve.wait_ge(G["top_turned"], 2)
            own.after(v.tensor_reduce(top16[0:16, 0:1], bank[6][0:16, 0:P], AX.X, ALU.max))
            v.tensor_scalar(top_bc[0:16, :], ident[0:16, 0:16], top16[0:16, 0:1], None, ALU.mult)\
                .then_inc(G["top_ready"], 1)
            dve.wait_ge(G["top_bc_ready"], 1)
            own.after(v.tensor_copy(top_bc, bank[6][:, P:P + 16]))
            own.after(v.tensor_tensor(top16[:, 0:8], top_bc[:, 0:8], top_bc[:, 8:16], ALU.add))
            own.after(v.tensor_reduce(flags[:, 3:4], top16[:, 0:8], AX.X, ALU.max))
            own.after(v.tensor_scalar(flags[:, 1:2], flags[:, 3:4], SPREAD, None, ALU.is_le))
            own.after(v.tensor_scalar(flags[:, 1:2], flags[:, 1:2], -1.0, 1.0, ALU.mult, ALU.add))
            v.tensor_copy(flags_i[0:1, 1:2], flags[0:1, 1:2]).then_inc(G["flags_ready"], 1)
            own.after(v.tensor_copy(top, bc(top_bc[:, 0:HEADS], 1, NB)))

            dve.wait_ge(G["flags_ready"], 1)
            general = dve.value_load(flags_i[0:1, 1:2], min_val=0, max_val=1)
            passes = dve.value_load(flags_i[0:1, 0:1], min_val=1, max_val=PASSES)
            with dve.If(general > 0):
                v.memset(max_acc, -3.0e38).then_inc(s_max["col"], 1)
                dve.sem_inc(s_max["free"], 1)
                with dve.Fori(0, NG) as g:
                    dve.wait_ge(s_max["turned"], g + 1)
                    for b in range(2):
                        ins = v.tensor_copy(elT_sb[:, 512 * b:512 * b + 512], bank[b][0:HEADS, :])
                    ins.then_inc(s_max["taken"], 1)
                    dve.wait_ge(s_max["taken"], g + 1)
                    hold(dve, s_max["dst"], g * 16 + 16)
                    with dve.Fori(0, GE) as e:
                        node = dve.value_load(dst_row[0:1, bass.ds(e, 1)], min_val=0, max_val=COLS - 1)
                        dve.wait_ge(s_max["col"], g * GE + e + 1)
                        v.tensor_tensor(max_acc[:, bass.ds(node, 1)], max_acc[:, bass.ds(node, 1)],
                                        elT_sb[:, bass.ds(e, 1)], ALU.max).then_inc(s_max["col"], 1)
                    dve.wait_ge(s_max["col"], (g + 1) * GE + 1)
                    dve.sem_inc(s_max["free"], 1)
                dve.wait_ge(s_max["col"], NG * GE + 1)
                with dve.Fori(0, NB) as b:
                    v.tensor_copy(stage_max, max_acc[:, bass.ds(b * P, P)]).then_inc(s_max["staged"], 1)
                    dve.wait_ge(s_max["blk"], b + 1)
                    v.tensor_copy(top[:, bass.ds(b, 1), :], bank[2][:, 0:HEADS].rearrange("p (a h) -> p a h", a=1))\
                        .then_inc(s_max["top"], 1)
                    dve.wait_ge(s_max["top"], b + 1)

            er_v = elr[:, :, 8:16]
            own.after(v.tensor_copy(erm[:, :, 0:8], er_v))
            own.after(v.tensor_tensor(top, top, er_v, ALU.add))
            v.scalar_tensor_tensor(out=erm[:, :, 8:16], in0=top, scalar=NEG_SLOPE, in1=top, op0=ALU.mult,
                                   op1=ALU.max).then_inc(G["er_ready_tab"], 1)
            dve.wait_ge(loads["bias"], 16)
            own.after(v.tensor_tensor(x_sb[:, :, :], x_sb[:, :, :], bc(bias_bc[:, :], 1, NB), ALU.add))

            own.after(v.tensor_reduce(least, wide[0:1, 0:NG].rearrange("p (q s) -> p q s", s=U), AX.X, ALU.min))
            shift = 1
            while shift < GI:
                own.after(v.tensor_tensor(least[:, 0:GI - shift], least[:, 0:GI - shift], least[:, shift:GI],
                                          ALU.min))
                shift *= 2
            own.after(v.tensor_scalar(ends, iota[0:1, 0:NB - 1], float(P), float(P), ALU.mult, ALU.add))
            own.after(v.tensor_tensor(past, bc(least, 2, NB - 1), bc(ends, 1, GI), ALU.is_ge))
            own.after(v.tensor_reduce(least, past, AX.X, ALU.add))
            v.memset(ready[:, 0:2], 0)
            v.tensor_copy(ready[:, 2:GI + 2], least).then_inc(G["ready_set"], 1)
            dve.wait_ge(G["ready_set"], 1)
            dve.wait_ge(G["er_stored"], 32)

            def targets(q, s):
                return dst_rel[:, bass.ds(q * U + s, 1), :].rearrange("p a t -> p (a t)")

            def next_pass(dve):
                own_pass.after(v.tensor_scalar(win_f[:, :], win_f[:, :], float(WIN), None, ALU.add))
                own_pass.after(v.tensor_copy(win_i[0:1, 1:NG + 1], win_f[0:1, :]))
                own_pass.after(v.tensor_scalar(dst_rel[:, 0:NG, :], dst_rel[:, 0:NG, :], -float(WIN), None, ALU.add))

            def one_hot(s, group):
                v.tensor_tensor(hot[:, s, :, :],
                                bc(dst_rel[:, bass.ds(group, 1), :].rearrange("p a t -> p (a t)"), 2, WIN),
                                bc(iota[:, :], 1, T), ALU.is_equal).then_inc(s_l1["hot"], 1)

            own_block = Own(dve, sem("own_block"))

            def divide_block(b):
                own_block.base, own_block.n = b * 7, 0
                dve.wait_ge(s_mid["agg"], b + 2)
                own_block.after(v.tensor_scalar(rden, bank[1][:, P:P + HEADS], TINY, None, ALU.max))
                own_block.after(v.reciprocal(rden, rden))
                own_block.after(v.tensor_tensor(
                    part_row.rearrange("p (h f) -> p h f", f=PER_HEAD),
                    bank[1][:, 0:P].rearrange("p (h f) -> p h f", f=PER_HEAD), bc(rden, 2, PER_HEAD), ALU.mult))
                dve.sem_inc(s_mid["agg_used"], 1)
                xs = x_sb[:, bass.ds(b, 1), :].rearrange("p a f -> p (a f)")
                own_block.after(v.tensor_tensor(xs, xs, part_row, ALU.add), hold)
                own_block.after(v.bn_stats(stats1, xs), hold)
                own_block.after(v.bn_aggr(mv1, stats1))
                own_block.after(v.tensor_copy(mv_all[:, bass.ds(b, 1), :].rearrange("p a f -> p (a f)"), mv1), hold)
                assert own_block.n == 7

            def add_sums(h, next_group, count):
                w0 = dve.value_load(win_i[0:1, bass.ds(next_group, 1)], min_val=0, max_val=COLS - WIN)
                dve.wait_ge(s_l1["agg"], count)
                dve.wait_ge(s_l1["added"], count)
                v.tensor_tensor(acc_a[:, bass.ds(w0, WIN)], acc_a[:, bass.ds(w0, WIN)],
                                bank[2 + h][:, 0:WIN], ALU.add)
                v.tensor_tensor(den_acc[:, bass.ds(w0, WIN)], den_acc[:, bass.ds(w0, WIN)],
                                bank[4 + h][0:HEADS, 0:WIN], ALU.add).then_inc(s_l1["added"], 1)

            dve.sem_inc(s_l1["added"], 1)
            dve.sem_inc(G["pass_set"], 1)
            own_pass, own_l1 = Own(dve, sem("own_pass1")), Own(dve, sem("own_l1"))
            with dve.Fori(0, passes) as k:
                hold(dve, s_l1["open"], k + 1)
                dve.wait_ge(s_l1["turned"], k * (NG + 1))
                one_hot(0, 0)
                with dve.Fori(0, GI) as q:
                    n = dve.snap(k * GI + q, min_val=0, max_val=PASSES * GI)
                    m = dve.snap(k * (NG + 1) + q * U, min_val=0, max_val=PASSES * (NG + 1))
                    own_l1.base, own_l1.n = n * (3 * U), 0

                    for s in range(U):
                        h = s % 2
                        dve.wait_ge(s_l1["er"], m + (s + 1))
                        dve.wait_ge(s_l1["rows"][s], q * (16 * T) + 16 * T)
                        dve.sem_inc(s_l1["landed"], 1)
                        er_e = bank[6 + h][:, 0:T * 16].rearrange("p (t f) -> p t f", f=16)
                        e3 = [e_sb[:, i, :].rearrange("p (t h) -> p t h", h=HEADS) for i in range(4)]
                        el_e = rows[:, s, :, HIDDEN:ZW]
                        own_l1.after(v.tensor_tensor(e3[0], el_e, er_e[:, :, 0:8], ALU.add))
                        own_l1.after(v.scalar_tensor_tensor(out=e3[1], in0=e3[0], scalar=NEG_SLOPE, in1=e3[0],
                                                            op0=ALU.mult, op1=ALU.max))
                        own_l1.after(v.tensor_tensor(e3[2], e3[1], er_e[:, :, 8:16], ALU.subtract))
                        v.tensor_scalar(e3[3], e3[2], 0.0, None, ALU.min).then_inc(s_l1["score"], 1)
                        one_hot((s + 1) % U, q * U + (s + 1))
                        dve.wait_ge(s_l1["exp"], n * U + (s + 1))
                        for hf in range(2):
                            ts = slice(hf * HT, hf * HT + HT)
                            ins = v.tensor_tensor(msg[:, h, ts, :].rearrange("p t (h f) -> p t h f", f=PER_HEAD),
                                                  rows[:, s, ts, 0:HIDDEN].rearrange("p t (h f) -> p t h f", f=PER_HEAD),
                                                  bc(a_sb[:, h, ts, :], 3, PER_HEAD), ALU.mult).then_inc(s_l1["msg"], 1)
                        dve.wait_ge(s_l1["msg"], (n * U + (s + 1)) * 2)
                        dve.sem_inc(s_l1["rows_free"], 1)
                        if s >= 1:
                            add_sums((s - 1) % 2, q * U + s, n * U + s)
                        else:
                            with dve.If(q > 0):
                                add_sums(1, q * U, n * U)
                        if s == 1:
                            blocks(dve, q + 1, divide_block)
                    assert own_l1.n == 3 * U
                add_sums(1, NG, (k + 1) * NG)
                own_pass.base, own_pass.n = k * 3, 0
                next_pass(dve)
                dve.sem_inc(G["pass_set"], 1)

            last_blocks(dve, divide_block)
            norm_scale(s_mid)

            node_rows(s_mid, HIDDEN)

            own.after(v.tensor_tensor(dst_rel[:, 0:NG, :], dst_rel[:, 0:NG, :],
                                      bc(win_f[:, :], 2, T), ALU.add))
            set_windows()
            def add_block(b):
                dve.wait_ge(s_out["agg"], b + 2)
                xs = x_sb[:, bass.ds(b, 1), :].rearrange("p a f -> p (a f)")
                v.tensor_tensor(xs, xs, bank[5][:, 0:P], ALU.add).then_inc(s_out["added"], 1)

            dve.wait_ge(zeroed, 13)
            dve.sem_inc(s_l2["added"], 1)
            own_pass, own_l2 = Own(dve, sem("own_pass2")), Own(dve, sem("own_l2"))
            with dve.Fori(0, passes) as k:
                hold(dve, s_l2["open"], k + 1)
                with dve.Fori(0, GI) as q:
                    n = dve.snap(k * GI + q, min_val=0, max_val=PASSES * GI)
                    own_l2.base, own_l2.n = n * (2 * U), 0

                    def add(s):
                        h = s % 2
                        w0 = dve.value_load(win_i[0:1, bass.ds(q * U + (s + 1), 1)], min_val=0, max_val=COLS - WIN)
                        dve.wait_ge(s_l2["half_free"], n * (2 * U) + (2 * s + 4))
                        dve.wait_ge(s_l2["added"], n * U + (s + 1))
                        v.tensor_tensor(acc_a[:, bass.ds(w0, WIN)], acc_a[:, bass.ds(w0, WIN)],
                                        bank[6 + h][:, 0:WIN], ALU.add)
                        v.tensor_tensor(acc_b[:, :, bass.ds(w0, WIN)], acc_b[:, :, bass.ds(w0, WIN)],
                                        bank[6 + h][:, WIN:4 * WIN].rearrange("p (k w) -> p k w", k=3), ALU.add)\
                            .then_inc(s_l2["added"], 1)

                    for s in range(U):
                        h = s % 2
                        dve.wait_ge(s_l2["in"][s], (n + k) * 32 + 32 if s < AHEAD else n * 32 + 32)
                        for hf in range(2):
                            ts = slice(hf * HT, hf * HT + HT)
                            own_l2.after(v.tensor_tensor(
                                eq[:, hf, :, :], bc(targets(q, s)[:, ts], 2, WIN),
                                bc(iota[:, :], 1, HT), ALU.is_equal))
                            dve.wait_ge(s_l2["half_free"], n * (2 * U) + (2 * s + hf + 1))
                            v.tensor_tensor(wy[:, hf, :, :].rearrange("p t (k w) -> p t k w", k=4),
                                            bc(eq[:, hf, :, :], 2, 4),
                                            bc(y_sb[:, s, ts, :], 3, WIN), ALU.mult)
                            if hf == 0:
                                dve.wait_ge(s_l2["tp"], n * U + k + (s + 1))
                                dve.wait_ge(s_l2["rows"][s], q * (16 * T) + 16 * T)
                                dve.sem_inc(s_l2["landed"], 1)
                            tp = pair[h][:, :, :].rearrange("p b (j f m) -> p (b j) f m", f=2, m=P)[:, :, hf, :]
                            g_v = rows[:, s, ts, 0:96].rearrange("p t (i u) -> p t i u", u=MUL)
                            for half, lo in ((0, 64), (1, 96)):
                                v.tensor_tensor(prod[:, hf, :, half, 0:96].rearrange("p t (i u) -> p t i u", u=MUL),
                                                g_v, bc(tp[:, :, lo:lo + 32], 2, 3), ALU.mult)
                            ins = v.tensor_tensor(prod[:, hf, :, :, 96:128], bc(rows[:, s, ts, 96:128], 2, 2),
                                                  tp[:, :, 0:64].rearrange("p t (i u) -> p t i u", u=MUL), ALU.mult)
                            ins.then_inc(s_l2["prod"], 1)
                            if s == 1 and hf == 0:
                                blocks(dve, q + 1, add_block)
                        dve.wait_ge(s_l2["prod"], n * (2 * U) + (2 * s + 2))
                        dve.sem_inc(s_l2["rows_free"], 1)
                        if s >= 1:
                            add(s - 1)
                    add(U - 1)
                    own_l2.n = 2 * U
                own_pass.base, own_pass.n = k * 3, 0
                next_pass(dve)

            last_blocks(dve, add_block)

        @block.tensor
        def _(pe):
            t = nc.tensor
            pe.wait_ge(loads["const"], 32)
            pe.wait_ge(loads["w"], 16)
            t.transpose(bank[7][:, 0:P], w_aug[:, 0:HIDDEN], ident[:, :]).then_inc(G["wT_ready"], 1)
            pe.wait_ge(G["red_ready"], 1)
            for n in range(4):
                mm = t.transpose(bank[5][0:NG2, n * P:n * P + P], redn[:, n // 2, (n % 2) * NG2:(n % 2) * NG2 + NG2],
                                 ident[:, :])
            mm.then_inc(G["red_turned"], 1)
            pe.wait_ge(G["attn_ready"], 3)
            pe.wait_ge(G["wT_copied"], 1)
            t.matmul(bank[7][:, 128:144], wT, attn_bd, start=True, stop=True).then_inc(G["wa_ready"], 1)
            pe.wait_ge(G["w_ready"], 1)

            def node_lin(s, weights, width):
                pe.sem_inc(s["turned"], BU)
                with pe.Fori(0, BI) as q:
                    for j in range(BU):
                        pe.wait_ge(s["norm"], q * BU + (j + 1))
                        t.transpose(bank[j // 4][:, (j % 4) * P:(j % 4) * P + P], h_sb[:, j, :], ident[:, :])\
                            .then_inc(s["turned"], 1)
                    for j in range(BU):
                        if j % 4 == 0:
                            pe.wait_ge(s["turned_sb"], q * 2 + (j // 4 + 1))
                        t.matmul(bank[2 + j // 3][:, (j % 3) * 144:(j % 3) * 144 + width], hT_sb[:, j, :], weights,
                                 start=True, stop=True).then_inc(s["lin"], 1)

            node_lin(s_in, w_aug[:, :], 144)

            pe.wait_ge(G["top_turned"], 1)
            t.transpose(bank[6][0:16, 0:P], top16, ident[:, :]).then_inc(G["top_turned"], 1)
            pe.wait_ge(G["top_ready"], 2)
            t.matmul(bank[6][:, P:P + 16], ones[:, :], top_bc[0:16, :], start=True, stop=True)\
                .then_inc(G["top_bc_ready"], 1)

            pe.wait_ge(G["flags_ready"], 1)
            general = pe.value_load(flags_i[0:1, 1:2], min_val=0, max_val=1)
            passes = pe.value_load(flags_i[0:1, 0:1], min_val=1, max_val=PASSES)
            with pe.If(general > 0):
                with pe.Fori(0, NG) as g:
                    pe.wait_ge(s_max["rows"], g * (16 * T) + 16 * T)
                    pe.wait_ge(s_max["free"], g + 1)
                    for i in range(T):
                        mm = t.transpose(bank[i // 4][0:HEADS, (i % 4) * P:(i % 4) * P + P],
                                         rows[:, 0, i, HIDDEN:ZW], ident[:, :])
                    mm.then_inc(s_max["turned"], 1)
                with pe.Fori(0, NB) as b:
                    hold(pe, s_max["staged"], b + 1)
                    t.transpose(bank[2][:, 0:HEADS], stage_max, ident[0:HEADS, 0:HEADS]).then_inc(s_max["blk"], 1)

            pe.wait_ge(G["ready_set"], 1)
            pe.sem_inc(s_mid["agg"], 1)

            def turn_sums(b):
                pe.wait_ge(s_mid["agg_staged"], b + 1)
                pe.wait_ge(s_mid["agg_used"], b)
                t.transpose(bank[1][:, 0:P], num_stage, ident[:, :])
                t.transpose(bank[1][:, P:P + HEADS], den_stage, ident[0:HEADS, 0:HEADS]).then_inc(s_mid["agg"], 1)

            def turn(s, m):
                pe.wait_ge(s_l1["hot"], m + 1)
                for j in range(HT):
                    mm = t.transpose(bank[0][0:2 * WIN, j * P:(j + 1) * P],
                                     hot[:, s, 2 * j:2 * j + 2, :].rearrange("p t w -> p (t w)"), ident[:, :])
                mm.then_inc(s_l1["turned"], 1)

            def targets_er(s, m, arrived):
                h = s % 2
                pe.wait_ge(s_l1["hot_turned"], m + 1)
                pe.wait_ge(s_l1["in"][s], arrived)
                for j in range(HT):
                    mm = t.matmul(bank[6 + h][:, j * 32:j * 32 + 32], hotT[0:2 * WIN, h, j * P:(j + 1) * P],
                                  er_win[0:2 * WIN, s, :], start=True, stop=True)
                mm.then_inc(s_l1["er"], 1)

            with pe.Fori(0, passes) as k:
                turn(0, k * (NG + 1))
                targets_er(0, k * (NG + 1), k * (32 * (GI + 1)) + 32)
                with pe.Fori(0, GI) as q:
                    n = pe.snap(k * GI + q, min_val=0, max_val=PASSES * GI)
                    m = pe.snap(k * (NG + 1) + q * U, min_val=0, max_val=PASSES * (NG + 1))

                    def sums(s, hf):
                        h = s % 2
                        for i in range(hf * HT, hf * HT + HT):
                            if i % HT == 0:
                                pe.wait_ge(s_l1["msg"], (n * U + s) * 2 + (i // HT + 1))
                            t.matmul(bank[2 + h][:, 0:WIN], msg[:, h, i, :], hot[:, s, i, :],
                                     start=(i == 0), stop=(i == T - 1))
                            mm = t.matmul(bank[4 + h][0:HEADS, 0:WIN], a_sb[:, h, i, :], hot[:, s, i, :],
                                          start=(i == 0), stop=(i == T - 1))
                        if hf == 1:
                            mm.then_inc(s_l1["agg"], 1)

                    for s in range(U):
                        turn((s + 1) % U, m + (s + 1))
                        sums(s, 0)
                        if s + 1 < AHEAD:
                            targets_er(s + 1, m + (s + 1), (n + k) * 32 + 32)
                        elif s + 1 < U:
                            targets_er(s + 1, m + (s + 1), n * 32 + 32)
                        else:
                            targets_er(0, m + U, (n + k) * 32 + 64)
                        if s == 1:
                            blocks(pe, q + 1, turn_sums)
                        sums(s, 1)

            last_blocks(pe, turn_sums)
            pe.wait_ge(G["up_w_ready"], 1)
            node_lin(s_mid, w_up[:, :], HIDDEN)

            pe.wait_ge(loads["mlp"], 160)
            pe.sem_inc(s_l2["half_free"], 2)

            def hidden1(s, arrived):
                pe.wait_ge(s_l2["in"][s], arrived)
                t.matmul(bank[4], a1_bd[:, :], ef_sb[:, s, :], start=True, stop=True).then_inc(s_l2["h1"], 1)

            def hidden2(m):
                pe.wait_ge(s_l2["h1_act"], m + 1)
                t.matmul(bank[5], a2_bd[:, :], h1_sb, start=True, stop=True).then_inc(s_l2["h2"], 1)

            def radial(m, h):
                pe.wait_ge(s_l2["h2_act"], m + 1)
                for j in range(HT):
                    mm = t.matmul(bank[2 * h + j // 2][:, (j % 2) * 256:(j % 2) * 256 + 256],
                                  h2_sb[:, h, j * P:(j + 1) * P], a3_bd[:, :], start=True, stop=True)
                mm.then_inc(s_l2["tp"], 1)

            pe.wait_ge(G["out_w_ready"], 3)
            pe.sem_inc(s_out["agg"], 1)

            def map_block(b):
                pe.wait_ge(s_out["agg_staged"], b + 1)
                pe.wait_ge(s_out["added"], b)
                for c in range(4):
                    mm = t.matmul(bank[5][:, 0:P], stage[:, c, :], wo_a[:, :] if c == 0 else wo_b[:, c - 1, :],
                                  start=(c == 0), stop=(c == 3), skip_group_check=True)
                mm.then_inc(s_out["agg"], 1)

            with pe.Fori(0, passes) as k:
                for s in range(AHEAD):
                    hidden1(s, k * (32 * (GI + 1)) + 32)
                    hidden2(k * (NG + AHEAD) + s)
                radial(k * (NG + AHEAD), 0)
                with pe.Fori(0, GI) as q:
                    n = pe.snap(k * GI + q, min_val=0, max_val=PASSES * GI)
                    m = pe.snap(k * (NG + AHEAD) + q * U, min_val=0, max_val=PASSES * (NG + AHEAD))

                    def sums(s, hf):
                        h = s % 2
                        pe.wait_ge(s_l2["prod"], n * (2 * U) + (2 * s + hf + 1))
                        for j in range(HT):
                            st, en = (hf + j == 0), (hf == 1 and j == HT - 1)
                            t.matmul(bank[6 + h][:, 0:WIN], prod[:, hf, j, 0, :], wy[:, hf, j, 0:WIN],
                                     start=st, stop=en, skip_group_check=True)
                            mm = t.matmul(bank[6 + h][:, WIN:4 * WIN], prod[:, hf, j, 1, :],
                                          wy[:, hf, j, WIN:4 * WIN], start=False, stop=en, skip_group_check=True)
                        mm.then_inc(s_l2["half_free"], 1)

                    for s in range(U):
                        radial(m + (s + 1), (s + 1) % 2)
                        if s == 1:
                            mapped = blocks(pe, q + 1, map_block)
                        hidden1((s + AHEAD) % U, n * 32 + 32 if s + AHEAD < U else (n + k) * 32 + 64)
                        sums(s, 0)
                        if s == 1:
                            pe.wait_ge(s_out["added"], mapped)
                        hidden2(m + (s + AHEAD))
                        sums(s, 1)

            last_blocks(pe, map_block)


def kernel(x, src, dst, edge_attr_4, edge_attr_8, **w):
    import numpy as np
    import concourse.bacc as bacc
    from concourse.bass_utils import run_bass_kernel_spmd

    extra = NG * GE - EDGES
    more = extra + AHEAD * GE
    arrays = {
        "x": np.concatenate([np.asarray(x), np.zeros((NB * P - NODES, HIDDEN), np.float32)]),
        "src": np.concatenate([np.asarray(src), np.zeros(extra, np.int32), np.asarray(src)[:U * GE]])
            .reshape(NG + U, P, T),
        "dst": np.ascontiguousarray(
            np.concatenate([np.asarray(dst), np.full(extra, PAD_DST, np.int32)]).reshape(NG, P, T).transpose(1, 0, 2)),
        "edge_y": np.concatenate([np.asarray(edge_attr_4), np.zeros((more, 4), np.float32)])
            .reshape(NG + AHEAD, P, T * 4),
        "edge_f": np.ascontiguousarray(
            np.concatenate([np.asarray(edge_attr_8), np.zeros((more, 8), np.float32)])
            .reshape(NG + AHEAD, P, 2, HT, 8).transpose(0, 2, 4, 3, 1)).reshape(NG + AHEAD, 16, HT * P),
    }
    for name, key in (("W", "L0_gnn_W"), ("attn_l", "L0_gnn_attn_l"), ("attn_r", "L0_gnn_attn_r"),
                      ("bias", "L0_gnn_bias"), ("W_up_s", "L1_gnn_W_up_s"), ("W_up_v", "L1_gnn_W_up_v"),
                      ("A1", "L1_gnn_A1"), ("b1", "L1_gnn_b1"), ("A2", "L1_gnn_A2"), ("b2", "L1_gnn_b2"),
                      ("A3", "L1_gnn_A3"), ("W_out_s", "L1_gnn_W_out_s"), ("W_out_v", "L1_gnn_W_out_v")):
        arrays[name] = np.ascontiguousarray(w[key])
    arrays["identity"] = np.concatenate([np.eye(P, dtype=np.float32),
                                         np.tile(np.arange(WIN + 2, dtype=np.float32), (P, 1))], axis=1)

    nc = bacc.Bacc("TRN2", target_bir_lowering=False, num_devices=1)
    args = [nc.dram_tensor(f"in_{n}", a.shape, mybir.dt.from_np(a.dtype), kind="ExternalInput").ap()
            for n, a in arrays.items()]
    out = nc.dram_tensor("out", (NODES, HIDDEN), F32, kind="ExternalOutput").ap()
    gnn_kernel(nc, *args, out)
    r = run_bass_kernel_spmd(nc, [{f"in_{n}": a for n, a in arrays.items()}], core_ids=[0])
    return r.results[0]["out"]
```
